# Optimizing a Trainium2 kernel written in Bass

```python
import numpy as np
import jax
import jax.numpy as jnp

def _softmax(x, axis=-1):
    return jax.nn.softmax(x, axis=axis)

def _gelu(x):
    return jax.nn.gelu(x, approximate=True)

def _silu(x):
    return jax.nn.silu(x)

def _sigmoid(x):
    return jax.nn.sigmoid(x)

def _layernorm(x, axis=-1, eps=1e-05):
    m = jnp.mean(x, axis=axis, keepdims=True)
    v = jnp.var(x, axis=axis, keepdims=True)
    return (x - m) / jnp.sqrt(v + eps)

def _scatter_add(tgt, idx, src, axis=0):
    return tgt.at[idx].add(src)

def _segment_sum(src, seg, n):
    return jax.ops.segment_sum(src, seg, n)
kernel_name = 'mk_xattn_ffn_d1_seqx_r4_0b6527'

def setup_inputs(seed: int=0):
    np.random.seed(seed)
    _w = jnp.asarray

    def _rec_inputs():
        import jax
        import jax.numpy as jnp
        _rk = jax.random.key(seed)
        x = -0.0002928 + 1 * jax.random.normal(jax.random.fold_in(_rk, 1), (8, 512, 256), jnp.float32)
        _lenS = 512 - jax.random.randint(jax.random.fold_in(_rk, 7), (8,), 0, max(1, 512 // 4) + 1, jnp.int32)
        _lenS2 = 512 - jax.random.randint(jax.random.fold_in(_rk, 8), (8,), 0, max(1, 512 // 4) + 1, jnp.int32)
        _ctx_1024P = jax.random.normal(jax.random.fold_in(_rk, 11), (8, 16, 256), jnp.float32)
        _ctx_1024c = jax.random.dirichlet(jax.random.fold_in(_rk, 511), 0.3 * jnp.ones((16,), jnp.float32), (8, 512))
        _ctx_1024t = jnp.einsum('bsk,bkd->bsd', _ctx_1024c, _ctx_1024P)
        _ctx_1024t = _ctx_1024t * jax.lax.rsqrt(jnp.mean(jnp.square(_ctx_1024t)) + 1e-12) * 0.953939
        ctx_1024 = -1.39393e-06 + 0.999914 * (_ctx_1024t + 0.3 * jax.random.normal(jax.random.fold_in(_rk, 611), (8, 512, 256), jnp.float32))
        return (x, ctx_1024)
    x, ctx_1024 = _rec_inputs()

    def _L0_xattn_setup():
        import jax, jax.numpy as jnp
        import numpy as np
        H = 16
        D_MODEL = 256
        BLOCK_SIZE = 64
        B, S = (2, 512)
        NEG = -65504.0
        key = jax.random.key(seed)
        ks = jax.random.split(key, 12)
        scale = 1.0 / np.sqrt(D_MODEL)
        inp = {'query': jax.random.normal(ks[0], (B, S, D_MODEL), jnp.float32), 'key': jax.random.normal(ks[1], (B, S, D_MODEL), jnp.float32), 'value': jax.random.normal(ks[2], (B, S, D_MODEL), jnp.float32), 'Wq': jax.random.normal(ks[3], (D_MODEL, D_MODEL), jnp.float32) * scale, 'bq': jnp.zeros((D_MODEL,), jnp.float32), 'Wk': jax.random.normal(ks[4], (D_MODEL, D_MODEL), jnp.float32) * scale, 'bk': jnp.zeros((D_MODEL,), jnp.float32), 'Wv': jax.random.normal(ks[5], (D_MODEL, D_MODEL), jnp.float32) * scale, 'bv': jnp.zeros((D_MODEL,), jnp.float32), 'Wo': jax.random.normal(ks[6], (D_MODEL, D_MODEL), jnp.float32) * scale, 'bo': jnp.zeros((D_MODEL,), jnp.float32)}
        return inp
    _L0_xattn_all = _L0_xattn_setup()
    _L0_xattn_in = {k: v for k, v in _L0_xattn_all.items() if k in ('Wq', 'bq', 'Wk', 'bk', 'Wv', 'bv', 'Wo', 'bo')}
    del _L0_xattn_all

    def _L0_ffn_setup():
        import jax, jax.numpy as jnp
        import numpy as np
        B, S, H, E, K, I = (4, 512, 256, 8, 2, 1024)
        GATE_EPS = 1e-06
        LN_EPS = 1e-05
        key = jax.random.key(seed)
        k0, k1, k2, k3 = jax.random.split(key, 4)
        x = jax.random.normal(k0, (B, S, H), jnp.float32)
        gate_w = jax.random.normal(k1, (E, H), jnp.float32) * np.float32(np.sqrt(2.0 / (H + E)))
        expert_bias = jnp.zeros((E,), jnp.float32)
        w_up = jax.random.normal(k2, (E, I, H), jnp.float32) * np.float32(np.sqrt(2.0 / (H + I)))
        w_down = jax.random.normal(k3, (E, H, I), jnp.float32) * np.float32(np.sqrt(2.0 / (H + I)))
        return {'x': x, 'gate_w': gate_w, 'expert_bias': expert_bias, 'w_up': w_up, 'w_down': w_down}
    _L0_ffn_all = _L0_ffn_setup()
    _L0_ffn_in = {k: v for k, v in _L0_ffn_all.items() if k in ('gate_w', 'expert_bias', 'w_up', 'w_down')}
    del _L0_ffn_all
    return {'x': x, 'ctx_1024': ctx_1024, 'L0_xattn_Wq': _L0_xattn_in['Wq'], 'L0_xattn_bq': _L0_xattn_in['bq'], 'L0_xattn_Wk': _L0_xattn_in['Wk'], 'L0_xattn_bk': _L0_xattn_in['bk'], 'L0_xattn_Wv': _L0_xattn_in['Wv'], 'L0_xattn_bv': _L0_xattn_in['bv'], 'L0_xattn_Wo': _L0_xattn_in['Wo'], 'L0_xattn_bo': _L0_xattn_in['bo'], 'L0_ffn_gate_w': _L0_ffn_in['gate_w'], 'L0_ffn_expert_bias': _L0_ffn_in['expert_bias'], 'L0_ffn_w_up': _L0_ffn_in['w_up'], 'L0_ffn_w_down': _L0_ffn_in['w_down']}

def reference(x, ctx_1024, L0_xattn_Wq, L0_xattn_bq, L0_xattn_Wk, L0_xattn_bk, L0_xattn_Wv, L0_xattn_bv, L0_xattn_Wo, L0_xattn_bo, L0_ffn_gate_w, L0_ffn_expert_bias, L0_ffn_w_up, L0_ffn_w_down):
    import jax
    import jax.numpy as jnp

    def _L0_xattn_ref(query, key, value, Wq, bq, Wk, bk, Wv, bv, Wo, bo):
        import jax, jax.numpy as jnp
        import numpy as np
        H = 16
        D_MODEL = 256
        BLOCK_SIZE = 64
        B, S = (2, 512)
        NEG = -65504.0
        b, s, d = query.shape
        dk = d // H

        def proj(x, W, bias):
            return (x @ W + bias).reshape(b, s, H, dk).transpose(0, 2, 1, 3)
        q = proj(query, Wq, bq)
        k = proj(key, Wk, bk)
        v = proj(value, Wv, bv)
        scores = jnp.einsum('bhqd,bhkd->bhqk', q, k) / jnp.sqrt(jnp.float32(dk))
        bid = jnp.arange(s) // BLOCK_SIZE
        attn_mask = jnp.where(bid[:, None] == bid[None, :], 0.0, NEG).astype(scores.dtype)
        scores = scores + attn_mask
        attn = jax.nn.softmax(scores, axis=-1)
        x = jnp.einsum('bhqk,bhkd->bhqd', attn, v)
        x = x.transpose(0, 2, 1, 3).reshape(b, s, d)
        return x @ Wo + bo

    def _L0_ffn_ref(x, gate_w, expert_bias, w_up, w_down):
        import jax, jax.numpy as jnp
        import numpy as np
        B, S, H, E, K, I = (4, 512, 256, 8, 2, 1024)
        GATE_EPS = 1e-06
        LN_EPS = 1e-05
        logits = jnp.einsum('bsh,eh->bse', x, gate_w) + expert_bias
        weights = jax.nn.softmax(logits, axis=-1)
        top_w, top_i = jax.lax.top_k(weights, K)
        top_w = top_w / (jnp.sum(top_w, axis=-1, keepdims=True) + GATE_EPS)
        sparse_w = jnp.sum(jax.nn.one_hot(top_i, E, dtype=weights.dtype) * top_w[..., None], axis=-2)
        out = jnp.zeros_like(x)
        for e in range(E):
            h = jax.nn.gelu(jnp.einsum('bsh,ih->bsi', x, w_up[e]), approximate=False)
            y = jnp.einsum('bsi,hi->bsh', h, w_down[e])
            out = out + sparse_w[..., e:e + 1] * y
        mu = jnp.mean(out, axis=-1, keepdims=True)
        var = jnp.mean(jnp.square(out - mu), axis=-1, keepdims=True)
        out = (out - mu) * jax.lax.rsqrt(var + LN_EPS)
        return out + x
    x = x + _L0_xattn_ref(_layernorm(x, axis=-1), ctx_1024, ctx_1024, L0_xattn_Wq, L0_xattn_bq, L0_xattn_Wk, L0_xattn_bk, L0_xattn_Wv, L0_xattn_bv, L0_xattn_Wo, L0_xattn_bo)
    x = x + _L0_ffn_ref(_layernorm(x, axis=-1), L0_ffn_gate_w, L0_ffn_expert_bias, L0_ffn_w_up, L0_ffn_w_down)
    return x

_drawn_inputs = setup_inputs


def setup_inputs(seed=0):
    import zlib

    import numpy as np

    out = dict(_drawn_inputs(seed))
    spreads = {'L0_xattn_bq': (0.0, 0.1),
     'L0_xattn_bk': (0.0, 0.1),
     'L0_xattn_bv': (0.0, 0.1),
     'L0_xattn_bo': (0.0, 0.1),
     'L0_ffn_expert_bias': (0.0, 0.1)}
    factors = {}
    for name, (base, spread) in spreads.items():
        noise = np.random.default_rng([zlib.crc32(name.encode()), seed]).standard_normal(out[name].shape)
        drawn = base * np.exp(spread * noise) if base else spread * noise
        out[name] = jnp.asarray(drawn.astype(out[name].dtype))
    for name, factor in factors.items():
        out[name] = (out[name] * factor).astype(out[name].dtype)
    return out
```

```python
from contextlib import ExitStack

import numpy as np

import concourse.bass as bass
from concourse import mybir

F32 = mybir.dt.float32
F16 = mybir.dt.float16
I32 = mybir.dt.int32
ALU = mybir.AluOpType
ACT = mybir.ActivationFunctionType
AX = mybir.AxisListType

P = 128
BATCH, SEQ, D = 8, 512, 256
TOKENS = BATCH * SEQ
TILES = TOKENS // P
HC = D // P
HEADS, DK, BLOCK = 16, 16, 64
PAIRS = HEADS // 2
STRIPS = 4
NB = P // BLOCK
E, I, TOPK = 8, 1024, 2
IC = I // P
SLOT_TILES = TOKENS * TOPK // P + E - 1
WSTEPS = 4 * E
WCOLS = HC * I // 2
EXPERT_COLS = HC * I
X_SCALE = 2048.0
W_SCALE = 256.0
G_SCALE = 256.0
LN_EPS = 1e-5
GATE_EPS = 1e-6
VCOLS = 2 * DK + 1

C_ID, C_TRI, C_ONES, C_IOTA, C_DESC, C_VAL, C_J128, C_MASK, C_PAD, C_END = np.cumsum(
    [0, P, P, P, P, E * TILES, TOPK * TILES, TILES, 2, SLOT_TILES]).tolist()


def constants():
    c = np.zeros((P, C_END), np.float32)
    p = np.arange(P)
    c[:, C_ID:C_ID + P] = np.eye(P)
    c[:, C_TRI:C_TRI + P] = p[:, None] < p[None, :]
    c[:, C_ONES:C_ONES + P] = 1
    c[:, C_IOTA:C_IOTA + P] = p[None, :]
    c[:, C_DESC:C_DESC + E * TILES] = (E - np.arange(E * TILES) // TILES)[None]
    g = np.arange(TOPK * TILES)
    c[:, C_VAL:C_VAL + g.size] = g[None] * P + p[:, None] - TOPK * TOKENS
    c[:, C_J128:C_J128 + TILES] = (P * np.arange(TILES))[None]
    c[:, C_MASK:C_MASK + 2] = (p[:, None] // DK % 2) == np.arange(2)[None]
    c[:, C_PAD:C_PAD + SLOT_TILES] = p[:, None] + P * (np.arange(SLOT_TILES) % 2)[None]
    return c


def program(nc, x, ctx_t, wq, wk, wv, wo, bq, bk, bv, bo, gate_t, gate_b, weights, consts, out):
    es = ExitStack()
    with es:
        def sb(name, shape, dt=F32):
            return es.enter_context(nc.sbuf_tensor(name, shape, dt))

        def sem(name):
            return es.enter_context(nc.semaphore(name))

        xn_rows = nc.dram_tensor("xn_rows", [TOKENS, D], F32, kind="Internal").ap()
        y_rows = nc.dram_tensor("y_rows", [TOPK * TOKENS + 2 * P, D], F32, kind="Internal").ap()

        resid = sb("resid", [P, TILES, D])
        w_hi = sb("w_hi", [P, 2 * E * EXPERT_COLS], F16)
        w_lo = sb("w_lo", [P, 2 * E * EXPERT_COLS], F16)
        cst = sb("cst", [P, C_END])
        gate_w = sb("gate_w", [P, HC, E])
        gate_bias = sb("gate_bias", [P, E])
        logits = sb("logits", [P, E, TILES])
        mix_w = sb("mix_w", [P, TOPK, TILES])
        slot_dest = sb("slot_dest", [P, SLOT_TILES], I32)
        slot_token = sb("slot_token", [P, SLOT_TILES], I32)
        slot_expert = sb("slot_expert", [P, SLOT_TILES], I32)

        ident = cst[:, C_ID:C_ID + P]

        AREA = 10700
        area = sb("area", [P, AREA])
        at = [0]

        def carve(cols, dt=F32):
            n = cols if dt != F16 else cols // 2
            v = area[:, at[0]:at[0] + n]
            at[0] += n
            assert at[0] <= AREA, at[0]
            return v if dt == F32 else v.bitcast(dt)

        wq_s, wk_s, wv_s, wo_s = (carve(HC * D).rearrange("p (c n) -> p c n", c=HC) for _ in range(4))
        bo_s = carve(D)
        bq_s, bk_s, bv_s = (carve(2) for _ in range(3))
        staging = [carve(WCOLS) for _ in range(2)]
        xn = carve(D)
        xn_t = carve(D).rearrange("p (c n) -> p c n", c=HC)
        ctx = [carve(D).rearrange("p (c n) -> p c n", c=HC) for _ in range(2)]
        q_m = carve(HC * 2 * P).rearrange("p (c b h n) -> p c b h n", c=HC, b=NB, h=2)
        k_t = carve(HC * P).rearrange("p (c n) -> p c n", c=HC)
        v_x = [carve(PAIRS * NB * VCOLS).rearrange("p (s c b x) -> p s c b x", s=STRIPS, c=HC, b=NB) for _ in range(2)]
        prob = carve(PAIRS * P)
        prob_t = carve(PAIRS * P).rearrange("p (h n) -> p h n", h=PAIRS)
        o_n = carve(D).rearrange("p (b n) -> p b n", b=NB)
        o_t = carve(D).rearrange("p (h n) -> p h n", h=2)
        xn2 = [carve(D) for _ in range(2)]
        xn2_t = carve(D).rearrange("p (c n) -> p c n", c=HC)
        row_max = carve(PAIRS * NB)
        o_sum = carve(PAIRS * NB)
        stats1, stats2 = carve(6), carve(6)
        mv1, mv2 = [carve(2) for _ in range(2)], [carve(2) for _ in range(2)]
        ve1, ve2 = carve(1), carve(1)
        rs1, rs2 = [carve(1) for _ in range(2)], [carve(1) for _ in range(2)]

        at[0] = 0
        def etv():
            return carve(E * TILES).rearrange("p (e t) -> p e t", e=E)
        lg_s, ex, eq, oh1, oh2, pos, base, tot, incl, mk, keep = (etv() for _ in range(11))
        lmax, lsum, lrec, m1, m2, i1, i2, den, drec = (carve(TILES) for _ in range(9))
        tiles_e, tin, tex = carve(E), carve(E), carve(E)
        pos_j = carve(TOPK * TILES)
        pos_i, tile_i, slot_i = (carve(TOPK * TILES).bitcast(I32) for _ in range(3))
        tile_f, slot_f = carve(TOPK * TILES), carve(TOPK * TILES)
        RG = 8
        is_slot = [carve(RG * P).rearrange("p (g s) -> p g s", g=RG) for _ in range(2)]
        is_tile = carve(RG * SLOT_TILES).rearrange("p (g s) -> p g s", g=RG)
        tile_val = [carve(RG * SLOT_TILES).rearrange("p (g s) -> p g s", g=RG) for _ in range(2)]
        ecmp = carve(SLOT_TILES * (E - 1)).rearrange("p (k e) -> p k e", e=E - 1)
        ecount = carve(SLOT_TILES)
        pad_p, dest_f, wrap1, wrap2, tok_f = (carve(SLOT_TILES) for _ in range(5))

        at[0] = 0
        xg = [carve(D) for _ in range(2)]
        xt_hi, xt_lo = ([carve(D, F16).rearrange("p (c n) -> p c n", c=HC) for _ in range(2)] for _ in range(2))
        g_s = [carve(I) for _ in range(2)]
        g_hi, g_lo = ([carve(I, F16).rearrange("p (c n) -> p c n", c=IC) for _ in range(2)] for _ in range(2))
        y_s = [carve(D) for _ in range(2)]
        gidx, didx = ([carve(1).bitcast(I32) for _ in range(2)] for _ in range(2))

        at[0] = 0
        CR = 4
        y_in = [carve(TOPK * D).rearrange("p (j n) -> p j n", j=TOPK) for _ in range(CR)]
        f_s = [carve(D) for _ in range(CR)]
        o_s = [carve(D) for _ in range(CR)]
        c_st = [carve(6) for _ in range(CR)]
        c_mv = [carve(2) for _ in range(CR)]
        c_ve = [carve(1) for _ in range(CR)]
        c_rs = [carve(1) for _ in range(CR)]
        neg_half, eps = sb("neg_half", [P, 1]), sb("eps", [P, 1])

        ps_a = es.enter_context(nc.psum_tensor("ps_a", [P, 4, 512], F32))
        ps_b = es.enter_context(nc.psum_tensor("ps_b", [P, 2, 512], F32))
        ps_c = es.enter_context(nc.psum_tensor("ps_c", [P, 2, 512], F32))
        ps_s = ps_a[:, :, 0:256].rearrange("p s (x k) -> p s x k", k=BLOCK)
        half_bank = lambda m, h: ps_c[:, m, h * 256:(h + 1) * 256].rearrange("p (c n) -> p c n", c=HC)
        ps_xt = ps_v = ps_ot = half_bank(0, 0)
        ps_x2t = half_bank(0, 1)
        ps_q, ps_k, ps_wo = half_bank(1, 0), half_bank(1, 1), half_bank(1, 0)
        ps_pt = ps_b[:, :, :].rearrange("p a (h n) -> p (a h) n", n=P)
        ps_o = ps_b[:, :, 0:4 * NB * VCOLS].rearrange("p a (y x) -> p a y x", x=VCOLS)
        ps_lg = ps_c[:, 1, 256:256 + E]
        ps_h = ps_a
        ps_y = ps_b
        ps_x = ps_c

        loaded = sem("loaded")
        x_in = [sem(f"x_in{i}") for i in range(2)]
        ctx_in = [sem(f"ctx_in{i}") for i in range(2)]
        w_in = [sem(f"w_in{i}") for i in range(2)]
        xn2_out = [sem(f"xn2_out{i}") for i in range(2)]
        zeroed = sem("zeroed")
        st1, mv1_r, ve1_r, rs1_r, xn_r = (sem(n) for n in ("st1", "mv1_r", "ve1_r", "rs1_r", "xn_r"))
        st2, mv2_r, ve2_r, rs2_r, xn2_r = (sem(n) for n in ("st2", "mv2_r", "ve2_r", "rs2_r", "xn2_r"))
        bo_added, x1_r, xn2_added = sem("bo_added"), sem("x1_r"), sem("xn2_added")
        xt_ps, xt_r = sem("xt_ps"), sem("xt_r")
        q_r, k_ps, k_r, v_ps, v_r = (sem(n) for n in ("q_r", "k_ps", "k_r", "v_ps", "v_r"))
        s_ps, max_r, sub_r, p_r, pt_ps, pt_r = (sem(n) for n in ("s_ps", "max_r", "sub_r", "p_r", "pt_ps", "pt_r"))
        o_ps, osum_r, o_r, ot_ps, ot_r, wo_ps = (sem(n) for n in ("o_ps", "osum_r", "o_r", "ot_ps", "ot_r", "wo_ps"))
        x2t_ps, x2t_r, lg_ps, lg_r = (sem(n) for n in ("x2t_ps", "x2t_r", "lg_ps", "lg_r"))
        w_scaled, w_hi_r, w_lo_r = sem("w_scaled"), sem("w_hi_r"), sem("w_lo_r")

        def here(j, u, skew):
            return 2 * j + (u + skew), j + (u + skew) // 2, (u + skew) % 2

        def flat2(v):
            return v.rearrange("p c n -> p (c n)")

        def valid(t):
            return not isinstance(t, int) or 0 <= t < TILES

        FIRST, LAST = 6, TILES - 4

        def steps(eng, lo, step):
            for i in range(lo, FIRST):
                step(i // 2, i % 2)
            with eng.Fori(FIRST // 2, LAST // 2) as j:
                step(j, 0)
                step(j, 1)
            for i in range(LAST, TILES + 5):
                step(i // 2, i % 2)

        def since(eng, s, count):
            if not isinstance(count, int) or count > 0:
                eng.wait_ge(s, count)

        passed = {n: sem(f"passed_{n}") for n in ("dve", "pool")}

        def settled(eng):
            eng.sem_inc(passed["dve" if eng.engine == nc.vector.engine else "pool"], 1)

        block = es.enter_context(nc.Block())

        small = [(cst[:, :], consts), (wq_s, wq), (wk_s, wk), (wv_s, wv), (wo_s, wo), (bq_s, bq), (bk_s, bk), (bv_s, bv),
                 (bo_s, bo), (gate_w[:, :, :], gate_t), (gate_bias[:, :], gate_b)]
        ALL_LOADED = 16 * len(small)

        rt = sem("rt")
        rt_shifted, rt_exp, rt_mask = sem("rt_shifted"), sem("rt_exp"), sem("rt_mask")
        rt_cnt = sem("rt_cnt")
        rt_grp = sem("rt_grp")
        rt_grp_used = sem("rt_grp_used")
        rt_slots = sem("rt_slots")
        routed = sem("routed")
        gat = [sem(f"gat{i}") for i in range(2)]
        scat = [sem(f"scat{i}") for i in range(2)]
        gidx_r, didx_r = sem("gidx_r"), sem("didx_r")
        gt_ps, xh_r, xl_r, h_ps, g_r, gh_r, gl_r, y_ps, y_r = (
            sem(n) for n in ("gt_ps", "xh_r", "xl_r", "h_ps", "g_r", "gh_r", "gl_r", "y_ps", "y_r"))
        power_r = sem("power_r")
        yin = [sem(f"yin{i}") for i in range(CR)]
        outs = [sem(f"outs{i}") for i in range(CR)]
        c_f0, c_f1, c_stats, c_mvr, c_ver, c_rsr, c_ap, c_out = (
            sem(n) for n in ("c_f0", "c_f1", "c_stats", "c_mvr", "c_ver", "c_rsr", "c_ap", "c_out"))

        MOE_FIRST, MOE_LAST = 4, 68
        COMB = [(t, t % CR) for t in range(TILES)]

        def moe_steps(eng, lo, step):
            for k in range(lo, MOE_FIRST):
                step(k // 2, k % 2)
            with eng.Fori(MOE_FIRST // 2, MOE_LAST // 2) as j:
                step(j, 0)
                step(j, 1)
            for k in range(MOE_LAST, SLOT_TILES + 1):
                step(k // 2, k % 2)

        def moe_valid(k):
            return not isinstance(k, int) or 0 <= k < SLOT_TILES

        def combine_steps(eng, step):
            with eng.Fori(0, TILES // CR) as j:
                for r in range(CR):
                    step(j, r)

        @block.sync
        def _(sp):
            for dst, src in small:
                sp.dma_start(dst, src).then_inc(loaded, 16)

            def step(j, u):
                t, half, b = here(j, u, 3)
                if valid(t):
                    since(sp, x_in[b], 16 * half)
                    sp.dma_start(resid[:, bass.ds(t, 1), :], x[bass.ds(t, 1)].rearrange("a p d -> p a d")).then_inc(x_in[b], 16)
                t, half, b = here(j, u, 1)
                if valid(t):
                    since(sp, v_ps, t - 1)
                    sp.dma_start(ctx[b], ctx_t[bass.ds(t, 1)].rearrange("a p c n -> p (a c) n")).then_inc(ctx_in[b], 16)
                t, half, b = here(j, u, 0)
                if valid(t):
                    since(sp, w_lo_r, t - 1)
                    sp.dma_start(staging[b], weights[bass.ds(t, 1)].rearrange("a p n -> p (a n)")).then_inc(w_in[b], 16)
                t, half, b = here(j, u, -3)
                if valid(t):
                    sp.wait_ge(xn2_r, t + 1)
                    sp.dma_start(xn_rows[bass.ds(t * P, P), :], xn2[b]).then_inc(xn2_out[b], 16)
            for i in range(-3, 0):
                step(i // 2, i % 2)
            steps(sp, 0, step)
            for b in range(2):
                sp.wait_ge(xn2_out[b], 16 * TILES // 2)

            sp.wait_ge(scat[0], 16 * ((SLOT_TILES + 1) // 2))
            sp.wait_ge(scat[1], 16 * (SLOT_TILES // 2))
            y_two = y_rows[0:TOPK * TOKENS, :].rearrange("(j t p) d -> t p j d", j=TOPK, p=P)

            def load(t, r):
                sp.dma_start(y_in[r], y_two[bass.ds(t, 1)].rearrange("a p j d -> p (a j) d")).then_inc(yin[r], 16)

            for r in range(CR):
                load(r, r)

            def store(t, r):
                sp.wait_ge(c_out, t + 1)
                sp.dma_start(out[bass.ds(t, 1)].rearrange("a p d -> p (a d)"), o_s[r]).then_inc(outs[r], 16)
            with sp.Fori(0, TILES // CR - 1) as j:
                for r in range(CR):
                    sp.wait_ge(c_f1, CR * j + (r + 1))
                    load(CR * j + (r + CR), r)
                    store(CR * j + r, r)
            for r in range(CR):
                store(TILES - CR + r, r)
            for r in range(CR):
                sp.wait_ge(outs[r], 16 * TILES // CR)

        @block.tensor
        def _(pe):
            pe.wait_ge(loaded, ALL_LOADED)
            pe.wait_ge(zeroed, 3)

            def step(j, u):
                t, half, b = here(j, u, 1)
                if valid(t):
                    pe.wait_ge(xn_r, t + 1)
                    since(pe, ot_r, 2 * (t - 3))
                    since(pe, x2t_r, t - 4)
                    since(pe, v_r, 2 * (t - 1))
                    for c in range(HC):
                        mm = pe.transpose(ps_xt[:, c, :], xn[:, c * P:(c + 1) * P], ident)
                    mm.then_inc(xt_ps, 1)
                t, half, b = here(j, u, 0)
                if valid(t):
                    pe.wait_ge(q_r, 4 * (t + 1))
                    pe.wait_ge(k_r, t + 1)
                    since(pe, sub_r, t)
                    for c in range(HC):
                        for n in range(NB):
                            for s in range(STRIPS):
                                mm = pe.matmul(ps_s[:, s, c * NB + n, :],
                                               q_m[32 * s:32 * s + 32, c, n].rearrange("p h q -> p (h q)"),
                                               k_t[32 * s:32 * s + 32, c, n * BLOCK:(n + 1) * BLOCK],
                                               start=True, stop=True)
                    mm.then_inc(s_ps, 1)
                t, half, b = here(j, u, -1)
                if valid(t):
                    pe.wait_ge(p_r, t + 1)
                    since(pe, o_r, 4 * t)
                    for h in range(PAIRS):
                        mm = pe.transpose(ps_pt[:, h, :], prob[:, h * P:(h + 1) * P], ident)
                    mm.then_inc(pt_ps, 1)
                t, half, b = here(j, u, 1)
                if valid(t):
                    pe.wait_ge(xt_r, t + 1)
                    since(pe, x1_r, t - 3)
                    since(pe, lg_r, t - 4)
                    for c in range(HC):
                        for k in range(HC):
                            mm = pe.matmul(ps_q[:, c, :], wq_s[:, k, c * P:(c + 1) * P], xn_t[:, k, :],
                                           start=(k == 0), stop=(k == HC - 1))
                    pe.wait_ge(ctx_in[b], 16 * (half + 1))
                    for c in range(HC):
                        for k in range(HC):
                            mm = pe.matmul(ps_k[:, c, :], wk_s[:, k, c * P:(c + 1) * P], ctx[b][:, k, :],
                                           start=(k == 0), stop=(k == HC - 1))
                    mm.then_inc(k_ps, 1)
                t, half, b = here(j, u, 0)
                if valid(t):
                    pe.wait_ge(ctx_in[b], 16 * (half + 1))
                    if valid(t + 1):
                        pe.wait_ge(xt_r, t + 2)
                    for k in range(HC):
                        mm = pe.matmul(flat2(ps_v), ctx[b][:, k, :], wv_s[:, k, :], start=(k == 0), stop=(k == HC - 1))
                    mm.then_inc(v_ps, 1)
                t, half, b = here(j, u, -1)
                if valid(t):
                    pe.wait_ge(pt_r, t + 1)
                    pe.wait_ge(v_r, 2 * (t + 1))
                    for h in range(PAIRS):
                        mm = pe.matmul(ps_o[:, h // 4, (h % 4) * NB:(h % 4 + 1) * NB, :], prob_t[:, h, :],
                                       v_x[b][:, h // HC, h % HC, :, :], start=True, stop=True)
                    mm.then_inc(o_ps, 1)
                t, half, b = here(j, u, -2)
                if valid(t):
                    pe.wait_ge(o_r, 4 * (t + 1))
                    if valid(t + 2):
                        pe.wait_ge(v_r, 2 * (t + 3))
                    for n in range(NB):
                        mm = pe.transpose(ps_ot[:, n, :], o_n[:, n, :], ident)
                    mm.then_inc(ot_ps, 1)
                t, half, b = here(j, u, -3)
                if valid(t):
                    pe.wait_ge(xn2_r, t + 1)
                    since(pe, x2t_r, t)
                    for c in range(HC):
                        mm = pe.transpose(ps_x2t[:, c, :], xn2[b][:, c * P:(c + 1) * P], ident)
                    mm.then_inc(x2t_ps, 1)
                t, half, b = here(j, u, -2)
                if valid(t):
                    pe.wait_ge(ot_r, 2 * (t + 1))
                    if valid(t + 3):
                        pe.wait_ge(k_r, t + 4)
                    since(pe, x1_r, t)
                    since(pe, lg_r, t - 1)
                    for h in range(2):
                        mm = pe.matmul(flat2(ps_wo), o_t[:, h, :], wo_s[:, h, :], start=(h == 0), stop=(h == 1))
                    mm.then_inc(wo_ps, 1)
                t, half, b = here(j, u, -3)
                if valid(t):
                    pe.wait_ge(x2t_r, t + 1)
                    pe.wait_ge(x1_r, t + 1)
                    since(pe, lg_r, t)
                    for k in range(HC):
                        mm = pe.matmul(ps_lg, xn2_t[:, k, :], gate_w[:, k, :], start=(k == 0), stop=(k == HC - 1))
                    mm.then_inc(lg_ps, 1)
            step(-1, 1)
            steps(pe, 0, step)

            pe.wait_ge(rt_mask, 1)
            pe.matmul(ps_b[:, 0, 0:E * TILES], cst[:, C_TRI:C_TRI + P], mk.rearrange("p e t -> p (e t)"), start=True, stop=True)
            pe.matmul(ps_b[:, 1, 0:E * TILES], cst[:, C_ONES:C_ONES + P], mk.rearrange("p e t -> p (e t)"),
                      start=True, stop=True).then_inc(rt_cnt, 1)
            for g in range(TOPK * TILES):
                if g % RG == 0:
                    pe.wait_ge(rt_grp, g // RG + 1)
                mm = pe.matmul(ps_c[:, 0, 0:SLOT_TILES], is_slot[g // RG % 2][:, g % RG, :], tile_val[g // RG % 2][:, g % RG, :],
                               start=(g == 0), stop=(g == TOPK * TILES - 1))
                if g % RG == RG - 1:
                    mm.then_inc(rt_grp_used, 1)

            pe.wait_ge(routed, 1)
            pe.wait_ge(w_lo_r, WSTEPS)

            def transpose_rows(k, half, b):
                pe.wait_ge(gat[b], 16 * (half + 1))
                since(pe, xl_r, k - 1)
                for c in range(HC):
                    mm = pe.transpose(ps_x[:, b, c * P:(c + 1) * P], xg[b][:, c * P:(c + 1) * P], ident)
                mm.then_inc(gt_ps, 1)

            def expert_of(k):
                e = pe.value_load(slot_expert[0:1, bass.ds(k, 1)], min_val=0, max_val=E - 1)
                return pe.snap(e * (2 * EXPERT_COLS))

            def up(k, b, first):
                pe.wait_ge(xl_r, k + 1)
                for ic in range(IC):
                    if ic % 4 == 0:
                        since(pe, g_r, 2 * (k - 2) + 1 + ic // 4)
                    n = 0
                    for hc in range(HC):
                        for w, r in ((w_hi, xt_hi), (w_hi, xt_lo), (w_lo, xt_hi)):
                            mm = pe.matmul(ps_h[:, 2 * b + ic // 4, (ic % 4) * P:(ic % 4 + 1) * P],
                                           w[:, bass.ds(first + (hc * I + ic * P), P)], r[b][:, hc, :],
                                           start=(n == 0), stop=(n == 3 * HC - 1))
                            n += 1
                    if ic % 4 == 3:
                        mm.then_inc(h_ps, 1)

            def down(k, b, first):
                since(pe, y_r, k - 1)
                n = 0
                for ic in range(IC):
                    if ic % 4 == 0:
                        pe.wait_ge(gl_r, 2 * k + 1 + ic // 4)
                    for g, w in ((g_hi, w_hi), (g_lo, w_hi), (g_hi, w_lo)):
                        mm = pe.matmul(ps_y[:, b, 0:D], g[b][:, ic, :], w[:, bass.ds(first + (EXPERT_COLS + ic * D), D)],
                                       start=(n == 0), stop=(n == 3 * IC - 1))
                        n += 1
                mm.then_inc(y_ps, 1)

            def moe(j, u):
                k, half, b = here(j, u, 2)
                if moe_valid(k):
                    transpose_rows(k, half, b)
                k, half, b = here(j, u, 1)
                if moe_valid(k):
                    up(k, b, expert_of(k))
                k, half, b = here(j, u, 0)
                if moe_valid(k):
                    down(k, b, expert_of(k))
            moe(-1, 0)
            moe(-1, 1)
            moe_steps(pe, 0, moe)

        @block.vector
        def _(dve):
            dve.memset(v_x[0], 0.0).then_inc(zeroed, 1)
            dve.memset(v_x[1], 0.0).then_inc(zeroed, 1)
            dve.wait_ge(zeroed, 2)
            for b in range(2):
                for n in range(NB):
                    r = slice(n * BLOCK, (n + 1) * BLOCK)
                    ins = dve.memset(v_x[b][r, :, :, n, 2 * DK:VCOLS].rearrange("p s c x -> p (s c) x"), 1.0)
            ins.then_inc(zeroed, 1)
            dve.wait_ge(loaded, ALL_LOADED)

            def step(j, u):
                t, half, b = here(j, u, -3)
                if valid(t):
                    dve.wait_ge(wo_ps, t + 1)
                    since(dve, lg_ps, t)
                    dve.wait_ge(bo_added, t + 1)
                    r = resid[:, bass.ds(t, 1), :].rearrange("p a d -> p (a d)")
                    dve.tensor_tensor(r, ps_wo.rearrange("p c n -> p (c n)"), r, ALU.add).then_inc(x1_r, 1)
                    since(dve, mv2_r, t)
                    dve.wait_ge(x1_r, t + 1)
                    settled(dve)
                    dve.bn_stats(stats2, r).then_inc(st2, 1)
                    since(dve, ve2_r, t - 1)
                    since(dve, xn2_r, t - 1)
                    dve.wait_ge(st2, t + 1)
                    settled(dve)
                    dve.bn_aggr(mv2[b], stats2).then_inc(mv2_r, 1)
                t, half, b = here(j, u, -4)
                if valid(t):
                    dve.wait_ge(lg_ps, t + 1)
                    dve.tensor_tensor(logits[:, :, bass.ds(t, 1)], ps_lg.unsqueeze(2), gate_bias[:, :].unsqueeze(2), ALU.add).then_inc(lg_r, 1)
                t, half, b = here(j, u, 0)
                if valid(t):
                    since(dve, sub_r, t)
                    dve.wait_ge(s_ps, t + 1)
                    dve.tensor_reduce(row_max.rearrange("p (s x) -> p s x", s=STRIPS), ps_s, AX.X, ALU.max).then_inc(max_r, 1)
                t, half, b = here(j, u, 3)
                if valid(t):
                    since(dve, mv1_r, t)
                    dve.wait_ge(x_in[b], 16 * (half + 1))
                    settled(dve)
                    dve.bn_stats(stats1, resid[:, bass.ds(t, 1), :].rearrange("p a d -> p (a d)")).then_inc(st1, 1)
                    since(dve, ve1_r, t - 1)
                    since(dve, xn_r, t - 1)
                    dve.wait_ge(st1, t + 1)
                    settled(dve)
                    dve.bn_aggr(mv1[b], stats1).then_inc(mv1_r, 1)
                t, half, b = here(j, u, 0)
                if valid(t):
                    dve.wait_ge(max_r, t + 1)
                    since(dve, pt_ps, t)
                    dve.tensor_tensor(prob.rearrange("p (s x k) -> p s x k", s=STRIPS, k=BLOCK), ps_s,
                                      row_max.rearrange("p (s x) -> p s x", s=STRIPS).unsqueeze(3).to_broadcast([P, STRIPS, HC * NB, BLOCK]),
                                      ALU.subtract).then_inc(sub_r, 1)
                t, half, b = here(j, u, -3)
                if valid(t):
                    dve.wait_ge(rs2_r, t + 1)
                    since(dve, xn2_out[b], 16 * half)
                    since(dve, x2t_ps, t - 1)
                    since(dve, xn2_added, t - 1)
                    dve.tensor_scalar(xn2[b], resid[:, bass.ds(t, 1), :].rearrange("p a d -> p (a d)"), mv2[b][:, 0:1], rs2[b],
                                      ALU.subtract, ALU.mult).then_inc(xn2_r, 1)
                t, half, b = here(j, u, 1)
                if valid(t):
                    dve.wait_ge(k_ps, t + 1)
                    for c in range(HC):
                        for h in range(2):
                            dve.tensor_scalar(q_m[:, c, :, h, :], ps_q[:, c, :].rearrange("p (b q) -> p b q", b=NB), bq_s[:, c:c + 1],
                                              cst[:, C_MASK + h:C_MASK + h + 1], ALU.add, ALU.mult).then_inc(q_r, 1)
                    dve.tensor_tensor(k_t, ps_k, bk_s.unsqueeze(2).to_broadcast([P, HC, P]), ALU.add).then_inc(k_r, 1)
                t, half, b = here(j, u, 2)
                if valid(t):
                    dve.wait_ge(rs1_r, t + 1)
                    since(dve, xt_ps, t)
                    dve.tensor_scalar(xn, resid[:, bass.ds(t, 1), :].rearrange("p a d -> p (a d)"), mv1[b][:, 0:1], rs1[b],
                                      ALU.subtract, ALU.mult).then_inc(xn_r, 1)
                t, half, b = here(j, u, -1)
                if valid(t):
                    dve.wait_ge(o_ps, t + 1)
                    since(dve, ot_ps, t)
                    since(dve, o_r, 4 * t)
                    dve.reciprocal(o_sum.rearrange("p (a y) -> p a y", a=2), ps_o[:, :, :, 2 * DK]).then_inc(osum_r, 1)
                    dve.wait_ge(osum_r, t + 1)
                    for h in range(2):
                        r = slice(h * BLOCK, (h + 1) * BLOCK)
                        for m in range(NB):
                            dve.tensor_tensor(o_n[r, m, :].rearrange("p (a y d) -> p a y d", a=2, d=DK),
                                              ps_o[r].rearrange("p a (y b) x -> p a y b x", b=NB)[:, :, :, m, h * DK:(h + 1) * DK],
                                              o_sum[r].rearrange("p (a y b) -> p a y b", a=2, b=NB)[:, :, :, m:m + 1].to_broadcast([BLOCK, 2, 4, DK]),
                                              ALU.mult).then_inc(o_r, 1)
            for i in range(-3, 0):
                step(i // 2, i % 2)
            steps(dve, 0, step)

            n = [0]

            def link(ins):
                n[0] += 1
                ins.then_inc(rt, 1)
                dve.wait_ge(rt, n[0])

            def over_e(v):
                return v.rearrange("p e t -> p t e")

            def per_t(v):
                return v.unsqueeze(1).to_broadcast([P, E, TILES])

            dve.wait_ge(lg_r, TILES)
            dve.wait_ge(ot_r, 2 * TILES)
            dve.wait_ge(x2t_r, TILES)
            dve.wait_ge(xn2_added, TILES)
            dve.wait_ge(w_lo_r, WSTEPS)
            dve.wait_ge(wo_ps, TILES)
            for b in range(2):
                dve.wait_ge(xn2_out[b], 16 * TILES // 2)
            desc = cst[:, C_DESC:C_DESC + E * TILES].rearrange("p (e t) -> p e t", e=E)
            link(dve.memset(keep, 1.0))
            link(dve.memset(keep[:, :, 0:1], 0.0))
            link(dve.tensor_reduce(lmax, over_e(logits[:, :, :]), AX.X, ALU.max))
            dve.tensor_tensor(lg_s, logits[:, :, :], per_t(lmax), ALU.subtract).then_inc(rt_shifted, 1)
            dve.wait_ge(rt_exp, 1)
            link(dve.tensor_reduce(lsum, over_e(ex), AX.X, ALU.add))
            link(dve.reciprocal(lrec, lsum))
            link(dve.tensor_tensor(ex, ex, per_t(lrec), ALU.mult))
            for m, i, oh in ((m1, i1, oh1), (m2, i2, oh2)):
                link(dve.tensor_reduce(m, over_e(ex), AX.X, ALU.max))
                link(dve.tensor_tensor(eq, ex, per_t(m), ALU.is_equal))
                link(dve.tensor_tensor(eq, eq, desc, ALU.mult))
                link(dve.tensor_reduce(i, over_e(eq), AX.X, ALU.max))
                link(dve.tensor_tensor(oh, desc, per_t(i), ALU.is_equal))
                if m is m1:
                    link(dve.scalar_tensor_tensor(ex, oh, -4.0, ex, ALU.mult, ALU.add))
            dve.tensor_tensor(mk, oh1, oh2, ALU.add).then_inc(rt_mask, 1)
            link(dve.scalar_tensor_tensor(den, m1, GATE_EPS, m2, ALU.add, ALU.add))
            link(dve.reciprocal(drec, den))
            link(dve.tensor_tensor(mix_w[:, 0, :], m1, drec, ALU.mult))
            link(dve.tensor_tensor(mix_w[:, 1, :], m2, drec, ALU.mult))
            dve.wait_ge(rt_cnt, 1)
            flat = lambda v: v.rearrange("p e t -> p (e t)")
            link(dve.tensor_copy(flat(tot), ps_b[:, 1, 0:E * TILES]))
            link(dve.tensor_tensor_scan(flat(incl), flat(keep), flat(tot), 0.0, ALU.mult, ALU.add))
            link(dve.tensor_tensor(base, incl, tot, ALU.subtract))
            j128 = cst[:, C_J128:C_J128 + TILES]
            link(dve.tensor_tensor(eq, incl[:, :, TILES - 1:TILES].to_broadcast([P, E, TILES]), per_t(j128), ALU.is_gt))
            link(dve.tensor_reduce(tiles_e, eq, AX.X, ALU.add))
            link(dve.tensor_tensor_scan(tin, cst[:, C_ONES:C_ONES + E], tiles_e, 0.0, ALU.mult, ALU.add))
            link(dve.tensor_tensor(tex, tin, tiles_e, ALU.subtract))
            link(dve.scalar_tensor_tensor(base, tex.unsqueeze(2).to_broadcast([P, E, TILES]), float(P), base, ALU.mult, ALU.add))
            link(dve.tensor_tensor(flat(pos), ps_b[:, 0, 0:E * TILES], flat(base), ALU.add))
            for c, oh in ((0, oh1), (1, oh2)):
                link(dve.tensor_tensor(eq, oh, pos, ALU.mult))
                link(dve.tensor_reduce(pos_j[:, c * TILES:(c + 1) * TILES], over_e(eq), AX.X, ALU.add))
            link(dve.tensor_copy(pos_i, pos_j))
            link(dve.tensor_scalar(tile_i, pos_i, P.bit_length() - 1, None, ALU.arith_shift_right))
            link(dve.tensor_scalar(slot_i, pos_i, P - 1, None, ALU.bitwise_and))
            link(dve.tensor_copy(tile_f, tile_i))
            link(dve.tensor_copy(slot_f, slot_i))
            for c in range(TOPK * TILES // RG):
                if c >= 2:
                    dve.wait_ge(rt_grp_used, c - 1)
                if c:
                    dve.wait_ge(rt_grp, c)
                g = slice(c * RG, (c + 1) * RG)
                dve.tensor_tensor(is_slot[c % 2], cst[:, C_IOTA:C_IOTA + P].unsqueeze(1).to_broadcast([P, RG, P]),
                                  slot_f[:, g].unsqueeze(2).to_broadcast([P, RG, P]), ALU.is_equal)
                link(dve.tensor_tensor(is_tile, cst[:, C_IOTA:C_IOTA + SLOT_TILES].unsqueeze(1).to_broadcast([P, RG, SLOT_TILES]),
                                       tile_f[:, g].unsqueeze(2).to_broadcast([P, RG, SLOT_TILES]), ALU.is_equal))
                dve.tensor_tensor(tile_val[c % 2], is_tile,
                                  cst[:, C_VAL + c * RG:C_VAL + (c + 1) * RG].unsqueeze(2).to_broadcast([P, RG, SLOT_TILES]),
                                  ALU.mult).then_inc(rt_grp, 1)
            link(dve.tensor_tensor(ecmp, tex[:, 1:E].unsqueeze(1).to_broadcast([P, SLOT_TILES, E - 1]),
                                   cst[:, C_IOTA:C_IOTA + SLOT_TILES].unsqueeze(2).to_broadcast([P, SLOT_TILES, E - 1]), ALU.is_le))
            link(dve.tensor_reduce(ecount, ecmp, AX.X, ALU.add))
            link(dve.tensor_copy(slot_expert[:, :], ecount))
            dve.wait_ge(rt_grp_used, TOPK * TILES // RG)
            ps_slot = ps_c[:, 0, 0:SLOT_TILES]
            link(dve.scalar_tensor_tensor(pad_p, ps_slot, 0.0, cst[:, C_PAD:C_PAD + SLOT_TILES], ALU.is_ge, ALU.mult))
            link(dve.scalar_tensor_tensor(dest_f, ps_slot, float(TOPK * TOKENS), pad_p, ALU.add, ALU.add))
            link(dve.tensor_copy(slot_dest[:, :], dest_f))
            link(dve.tensor_scalar(wrap1, dest_f, float(TOKENS), -float(TOKENS), ALU.is_ge, ALU.mult))
            link(dve.tensor_scalar(wrap2, dest_f, float(TOPK * TOKENS), -float(TOKENS), ALU.is_ge, ALU.mult))
            link(dve.tensor_tensor(tok_f, dest_f, wrap1, ALU.add))
            link(dve.tensor_tensor(tok_f, tok_f, wrap2, ALU.add))
            dve.tensor_copy(slot_token[:, :], tok_f).then_inc(routed, 1)

            dve.wait_ge(routed, 1)

            def moe(j, u):
                k, half, b = here(j, u, 2)
                if moe_valid(k):
                    dve.wait_ge(gt_ps, k + 1)
                    since(dve, h_ps, 2 * (k - 1))
                    src = ps_x[:, b, 0:D].rearrange("p (c n) -> p c n", c=HC)
                    dve.tensor_scalar(xt_hi[b], src, X_SCALE, None, ALU.mult).then_inc(xh_r, 1)
                    dve.wait_ge(xh_r, k + 1)
                    dve.scalar_tensor_tensor(xt_lo[b], src, X_SCALE, xt_hi[b], ALU.mult, ALU.subtract).then_inc(xl_r, 1)
                k, half, b = here(j, u, 1)
                if moe_valid(k):
                    since(dve, y_ps, k - 1)
                    for m in range(2):
                        g = slice(m * I // 2, (m + 1) * I // 2)
                        c = slice(m * IC // 2, (m + 1) * IC // 2)
                        src = g_s[b][:, g].rearrange("p (c n) -> p c n", n=P)
                        dve.wait_ge(g_r, 2 * k + 1 + m)
                        dve.tensor_scalar(g_hi[b][:, c, :], src, G_SCALE, None, ALU.mult).then_inc(gh_r, 1)
                        dve.wait_ge(gh_r, 2 * k + 1 + m)
                        dve.scalar_tensor_tensor(g_lo[b][:, c, :], src, G_SCALE, g_hi[b][:, c, :], ALU.mult, ALU.subtract).then_inc(gl_r, 1)
            moe(-1, 0)
            moe(-1, 1)
            moe_steps(dve, 0, moe)

            def combine(j, r):
                t = CR * j + r
                dve.wait_ge(c_f0, t + 1)
                w = mix_w[:, 1, bass.ds(t, 1)]
                dve.scalar_tensor_tensor(f_s[r], y_in[r][:, 1, :], w, f_s[r], ALU.mult, ALU.add).then_inc(c_f1, 1)
                dve.wait_ge(c_f1, t + 1)
                settled(dve)
                dve.bn_stats(c_st[r], f_s[r]).then_inc(c_stats, 1)
                dve.wait_ge(c_stats, t + 1)
                settled(dve)
                dve.bn_aggr(c_mv[r], c_st[r]).then_inc(c_mvr, 1)

            def finish(j, r):
                t = CR * j + r
                dve.wait_ge(c_rsr, t + 1)
                dve.tensor_scalar(f_s[r], f_s[r], c_mv[r][:, 0:1], c_rs[r], ALU.subtract, ALU.mult).then_inc(c_ap, 1)
                dve.wait_ge(c_ap, t + 1)
                since(dve, outs[r], 16 * j)
                dve.tensor_tensor(o_s[r], f_s[r], resid[:, bass.ds(t, 1), :].rearrange("p a d -> p (a d)"), ALU.add).then_inc(c_out, 1)
            for t in range(2 * CR):
                combine(t // CR, t % CR)
                if t:
                    finish((t - 1) // CR, (t - 1) % CR)
            with dve.Fori(2, TILES // CR) as j:
                for r in range(CR):
                    combine(j, r)
                    finish(j if r else j - 1, (r - 1) % CR)
            finish(TILES // CR - 1, CR - 1)

        @block.scalar
        def _(act):
            act.wait_ge(loaded, ALL_LOADED)
            act.wait_ge(zeroed, 3)

            def step(j, u):
                t, half, b = here(j, u, 1)
                if valid(t):
                    act.wait_ge(xt_ps, t + 1)
                    since(act, k_ps, t)
                    act.activation(xn_t, ps_xt, ACT.Copy).then_inc(xt_r, 1)
                t, half, b = here(j, u, 0)
                if valid(t):
                    act.wait_ge(w_in[b], 16 * (half + 1))
                    act.activation(staging[b], staging[b], ACT.Copy, scale=W_SCALE).then_inc(w_scaled, 1)
                t, half, b = here(j, u, -1)
                if valid(t):
                    act.wait_ge(pt_ps, t + 1)
                    since(act, o_ps, t)
                    act.activation(prob_t, ps_pt, ACT.Copy).then_inc(pt_r, 1)
                t, half, b = here(j, u, 0)
                if valid(t):
                    act.wait_ge(v_ps, t + 1)
                    since(act, o_ps, t - 1)
                    for n in range(NB):
                        r = slice(n * BLOCK, (n + 1) * BLOCK)
                        act.activation(v_x[b][r, :, :, n, 0:2 * DK],
                                       ps_v[r].rearrange("p c (s d) -> p s c d", s=STRIPS), ACT.Copy).then_inc(v_r, 1)
                    act.wait_ge(sub_r, t + 1)
                    act.activation(prob, prob, ACT.Exp, scale=DK ** -0.5).then_inc(p_r, 1)
                t, half, b = here(j, u, -2)
                if valid(t):
                    act.wait_ge(ot_ps, t + 1)
                    since(act, x2t_ps, t)
                    since(act, wo_ps, t)
                    for h in range(2):
                        act.activation(o_t[:, h, :].rearrange("p (b q) -> p b q", b=NB), ps_ot[:, :, h * BLOCK:(h + 1) * BLOCK],
                                       ACT.Identity, bias=bv_s[:, h:h + 1]).then_inc(ot_r, 1)
                t, half, b = here(j, u, -3)
                if valid(t):
                    act.wait_ge(x2t_ps, t + 1)
                    since(act, lg_ps, t)
                    act.activation(xn2_t, ps_x2t, ACT.Copy).then_inc(x2t_r, 1)
            step(-1, 1)
            steps(act, 0, step)

            act.wait_ge(rt_shifted, 1)
            act.activation(ex, lg_s, ACT.Exp).then_inc(rt_exp, 1)
            act.wait_ge(routed, 1)

            def moe(j, u):
                k, half, b = here(j, u, 1)
                if moe_valid(k):
                    for m in range(2):
                        act.wait_ge(h_ps, 2 * k + 1 + m)
                        since(act, gl_r, 2 * (k - 2) + 1 + m)
                        act.activation(g_s[b][:, m * I // 2:(m + 1) * I // 2], ps_h[:, 2 * b + m, :], ACT.Gelu,
                                       scale=1.0 / (X_SCALE * W_SCALE)).then_inc(g_r, 1)
                k, half, b = here(j, u, 0)
                if moe_valid(k):
                    act.wait_ge(y_ps, k + 1)
                    since(act, scat[b], 16 * half)
                    act.activation(y_s[b], ps_y[:, b, 0:D], ACT.Copy, scale=1.0 / (G_SCALE * W_SCALE)).then_inc(y_r, 1)
            moe(-1, 1)
            moe_steps(act, 0, moe)

            def combine(j, r):
                t = CR * j + r
                act.wait_ge(yin[r], 16 * (j + 1))
                if not isinstance(j, int):
                    act.wait_ge(c_out, t - CR + 1)
                act.activation(f_s[r], y_in[r][:, 0, :], ACT.Copy, scale=mix_w[:, 0, bass.ds(t, 1)]).then_inc(c_f0, 1)
            for r in range(CR):
                combine(0, r)
            with act.Fori(1, TILES // CR) as j:
                for r in range(CR):
                    combine(j, r)

        @block.gpsimd
        def _(pool):
            pool.memset(neg_half[:, :], -0.5).then_inc(power_r, 1)
            pool.memset(eps[:, :], LN_EPS).then_inc(power_r, 1)
            pool.wait_ge(power_r, 2)
            pool.wait_ge(loaded, ALL_LOADED)

            def rstd(t, mv, ve, ve_r, rs, rs_r):
                pool.tensor_tensor(ve, mv[:, 1:2], eps[:, :], ALU.add).then_inc(ve_r, 1)
                pool.wait_ge(ve_r, t + 1)
                pool.tensor_tensor(rs, ve, neg_half[:, :], ALU.pow).then_inc(rs_r, 1)

            def step(j, u):
                t, half, b = here(j, u, -3)
                if valid(t):
                    pool.wait_ge(mv2_r, t + 1)
                    since(pool, rs2_r, t)
                    since(pool, xn2_r, t - 1)
                    rstd(t, mv2[b], ve2, ve2_r, rs2[b], rs2_r)
                t, half, b = here(j, u, 3)
                if valid(t):
                    pool.wait_ge(mv1_r, t + 1)
                    since(pool, xn_r, t - 1)
                    since(pool, rs1_r, t)
                    rstd(t, mv1[b], ve1, ve1_r, rs1[b], rs1_r)
                t, half, b = here(j, u, 1)
                if valid(t):
                    pool.wait_ge(xn_r, t + 1)
                    r = resid[:, bass.ds(t, 1), :].rearrange("p a d -> p (a d)")
                    pool.tensor_tensor(r, r, bo_s, ALU.add).then_inc(bo_added, 1)
                t, half, b = here(j, u, 0)
                if valid(t):
                    cols = bass.ds(t * WCOLS, WCOLS)
                    pool.wait_ge(w_scaled, t + 1)
                    pool.tensor_copy(w_hi[:, cols], staging[b]).then_inc(w_hi_r, 1)
                    pool.wait_ge(w_hi_r, t + 1)
                    pool.tensor_tensor(w_lo[:, cols], staging[b], w_hi[:, cols], ALU.subtract).then_inc(w_lo_r, 1)
                t, half, b = here(j, u, -3)
                if valid(t):
                    pool.wait_ge(xn2_r, t + 1)
                    r = resid[:, bass.ds(t, 1), :].rearrange("p a d -> p (a d)")
                    pool.tensor_tensor(r, r, xn2[b], ALU.add).then_inc(xn2_added, 1)
            for i in range(-3, 0):
                step(i // 2, i % 2)
            steps(pool, 0, step)

            pool.wait_ge(routed, 1)
            for b in range(2):
                pool.wait_ge(xn2_out[b], 16 * TILES // 2)

            def moe(j, u):
                k, half, b = here(j, u, 3)
                if moe_valid(k):
                    since(pool, gt_ps, k - 1)
                    since(pool, gat[b], 16 * half)
                    pool.tensor_copy(gidx[b], slot_token[:, bass.ds(k, 1)]).then_inc(gidx_r, 1)
                    pool.wait_ge(gidx_r, k + 1)
                    settled(pool)
                    pool.indirect_dma_start(xg[b], None, xn_rows[:, :], bass.IndirectOffsetOnAxis(ap=gidx[b], axis=0)).then_inc(gat[b], 16)
                k, half, b = here(j, u, -1)
                if moe_valid(k):
                    since(pool, scat[b], 16 * half)
                    pool.tensor_copy(didx[b], slot_dest[:, bass.ds(k, 1)]).then_inc(didx_r, 1)
                    pool.wait_ge(didx_r, k + 1)
                    pool.wait_ge(y_r, k + 1)
                    settled(pool)
                    pool.indirect_dma_start(y_rows[:, :], bass.IndirectOffsetOnAxis(ap=didx[b], axis=0), y_s[b], None).then_inc(scat[b], 16)
            for k in range(-3, 0):
                moe(k // 2, k % 2)
            moe_steps(pool, 0, moe)

            def combine(j, r):
                t = CR * j + r
                pool.wait_ge(c_mvr, t + 1)
                rstd(t, c_mv[r], c_ve[r], c_ver, c_rs[r], c_rsr)
            combine_steps(pool, combine)


def kernel(x, ctx_1024, L0_xattn_Wq, L0_xattn_bq, L0_xattn_Wk, L0_xattn_bk, L0_xattn_Wv, L0_xattn_bv, L0_xattn_Wo, L0_xattn_bo,
           L0_ffn_gate_w, L0_ffn_expert_bias, L0_ffn_w_up, L0_ffn_w_down):
    import concourse.bacc as bacc
    from concourse.bass_utils import run_bass_kernel_spmd

    rows = lambda w: np.asarray(w).reshape(HC, P, -1).transpose(1, 0, 2)
    heads = (HC, STRIPS, 2, DK)
    up = np.asarray(L0_ffn_w_up).transpose(0, 2, 1).reshape(E, HC, P, I)
    down = np.asarray(L0_ffn_w_down).transpose(0, 2, 1).reshape(E, 2, IC // 2, P, D).transpose(0, 1, 3, 2, 4).reshape(E, 2, P, WCOLS)
    arrays = {
        "x_in": np.asarray(x).reshape(TILES, P, D),
        "ctx_t": np.asarray(ctx_1024).reshape(TILES, P, HC, P).transpose(0, 3, 2, 1),
        "wq": rows(L0_xattn_Wq), "wk": rows(L0_xattn_Wk), "wv": rows(L0_xattn_Wv),
        "wo": np.asarray(L0_xattn_Wo).reshape(*heads, D).transpose(1, 0, 3, 2, 4).reshape(P, 2, D),
        "bq": np.asarray(L0_xattn_bq).reshape(HC, P).T, "bk": np.asarray(L0_xattn_bk).reshape(HC, P).T,
        "bv": np.asarray(L0_xattn_bv).reshape(heads).transpose(1, 0, 3, 2).reshape(P, 2),
        "bo": np.broadcast_to(np.asarray(L0_xattn_bo), (P, D)),
        "gate_t": rows(np.asarray(L0_ffn_gate_w).T), "gate_b": np.broadcast_to(np.asarray(L0_ffn_expert_bias), (P, E)),
        "weights": np.concatenate([up, down], 1).reshape(WSTEPS, P, WCOLS),
        "consts": constants(),
    }
    arrays = {n: np.ascontiguousarray(a) for n, a in arrays.items()}
    nc = bacc.Bacc("TRN2", target_bir_lowering=False, num_devices=1)
    args = [nc.dram_tensor(n, a.shape, mybir.dt.from_np(a.dtype), kind="ExternalInput").ap() for n, a in arrays.items()]
    out = nc.dram_tensor("out", (TILES, P, D), F32, kind="ExternalOutput").ap()
    program(nc, *args, out)
    r = run_bass_kernel_spmd(nc, [arrays], core_ids=[0])
    return r.results[0]["out"].reshape(BATCH, SEQ, D)
```

```python
from contextlib import ExitStack

import numpy as np

import concourse.bass as bass
from concourse import mybir

F32 = mybir.dt.float32
F16 = mybir.dt.float16
I32 = mybir.dt.int32
ALU = mybir.AluOpType
ACT = mybir.ActivationFunctionType
AX = mybir.AxisListType

P = 128
BATCH, SEQ, D = 8, 512, 256
TOKENS = BATCH * SEQ
TILES = TOKENS // P
HC = D // P
HEADS, DK, BLOCK = 16, 16, 64
PAIRS = HEADS // 2
STRIPS = 4
NB = P // BLOCK
E, I, TOPK = 8, 1024, 2
IC = I // P
SUBS = 2
SLOTS = SUBS * P
SLOT_TILES = TOKENS * TOPK // SLOTS + E - 1
UNITS = SUBS * SLOT_TILES
WSTEPS = 4 * E
WCOLS = HC * I // 2
EXPERT_COLS = HC * I
X_SCALE = 2048.0
W_SCALE = 256.0
G_SCALE = 256.0
LN_EPS = 1e-5
GATE_EPS = 1e-6
VCOLS = 2 * DK + 1

C_ID, C_MASK, C_END = np.cumsum([0, P, 2]).tolist()
R_TRI, R_ONES, R_IOTA, R_DESC, R_VAL, R_STEP, R_PAD, R_END = np.cumsum(
    [0, P, P, P, E * TILES, TOPK * TILES, TILES, UNITS]).tolist()


def constants():
    c, r = np.zeros((P, C_END), np.float32), np.zeros((P, R_END), np.float32)
    p = np.arange(P)
    c[:, C_ID:C_ID + P] = np.eye(P)
    c[:, C_MASK:C_MASK + 2] = (p[:, None] // DK % 2) == np.arange(2)[None]
    r[:, R_TRI:R_TRI + P] = p[:, None] < p[None, :]
    r[:, R_ONES:R_ONES + P] = 1
    r[:, R_IOTA:R_IOTA + P] = p[None, :]
    r[:, R_DESC:R_DESC + E * TILES] = (E - np.arange(E * TILES) // TILES)[None]
    g = np.arange(TOPK * TILES)
    r[:, R_VAL:R_VAL + g.size] = g[None] * P + p[:, None] - TOPK * TOKENS
    r[:, R_STEP:R_STEP + TILES] = (SLOTS * np.arange(TILES))[None]
    r[:, R_PAD:R_PAD + UNITS] = p[:, None] + P * (np.arange(UNITS) % (2 * SUBS))[None]
    return c, r


def program(nc, x, ctx_t, wq, wk, wv, wo, bq, bk, bv, bo, gate_t, gate_b, weights, consts, route_consts, out):
    es = ExitStack()
    with es:
        def sb(name, shape, dt=F32):
            return es.enter_context(nc.sbuf_tensor(name, shape, dt))

        def sem(name):
            return es.enter_context(nc.semaphore(name))

        xn_rows = nc.dram_tensor("xn_rows", [TOKENS, D], F32, kind="Internal").ap()
        y_rows = nc.dram_tensor("y_rows", [TOPK * TOKENS + 2 * SLOTS, D], F32, kind="Internal").ap()

        resid = sb("resid", [P, TILES, D])
        w_hi = sb("w_hi", [P, 2 * E * EXPERT_COLS], F16)
        w_lo = sb("w_lo", [P, 2 * E * EXPERT_COLS], F16)
        cst = sb("cst", [P, C_END])
        gate_w = sb("gate_w", [P, HC, E])
        gate_bias = sb("gate_bias", [P, E])
        logits = sb("logits", [P, E, TILES])
        mix_w = sb("mix_w", [P, TOPK, TILES])
        slot_dest = sb("slot_dest", [P, UNITS], I32)
        slot_token = sb("slot_token", [P, UNITS], I32)
        slot_expert = sb("slot_expert", [P, SLOT_TILES], I32)

        ident = cst[:, C_ID:C_ID + P]

        AREA = 11500
        area = sb("area", [P, AREA])
        at = [0]

        def carve(cols, dt=F32):
            n = cols if dt != F16 else cols // 2
            v = area[:, at[0]:at[0] + n]
            at[0] += n
            assert at[0] <= AREA, at[0]
            return v if dt == F32 else v.bitcast(dt)

        wq_s, wk_s, wv_s, wo_s = (carve(HC * D).rearrange("p (c n) -> p c n", c=HC) for _ in range(4))
        bo_s = carve(D)
        bq_s, bk_s, bv_s = (carve(2) for _ in range(3))
        staging = [carve(WCOLS) for _ in range(2)]
        xn = carve(D)
        xn_t = xn2_t = carve(D).rearrange("p (c n) -> p c n", c=HC)
        ctx = [carve(D).rearrange("p (c n) -> p c n", c=HC) for _ in range(2)]
        q_m = carve(HC * 2 * P).rearrange("p (c b h n) -> p c b h n", c=HC, b=NB, h=2)
        q_b = carve(HC * P).rearrange("p (c n) -> p c n", c=HC)
        k_bd = carve(HC * NB * STRIPS * BLOCK).rearrange("p (c b s k) -> p c b s k", c=HC, b=NB, s=STRIPS)
        v_x = [carve(PAIRS * NB * VCOLS).rearrange("p (s c b x) -> p s c b x", s=STRIPS, c=HC, b=NB) for _ in range(2)]
        prob = carve(PAIRS * P)
        prob_t = carve(PAIRS * P).rearrange("p (h n) -> p h n", h=PAIRS)
        o_n = carve(D).rearrange("p (b n) -> p b n", b=NB)
        o_t = carve(D).rearrange("p (h n) -> p h n", h=2)
        xn2 = carve(D)
        row_max = carve(PAIRS * NB)
        o_sum = carve(PAIRS * NB)
        stats1, stats2 = carve(6), carve(6)
        mv1, mv2 = [carve(2) for _ in range(2)], [carve(2) for _ in range(2)]
        ve1, ve2 = carve(1), carve(1)
        rs1, rs2 = [carve(1) for _ in range(2)], [carve(1) for _ in range(2)]

        at[0] = 0
        rc = carve(R_END)

        def etv():
            return carve(E * TILES).rearrange("p (e t) -> p e t", e=E)
        lg_s, ex, eq, oh1, oh2, pos, base, tot, incl, mk, keep = (etv() for _ in range(11))
        lmax, lsum, lrec, m1, m2, i1, i2, den, drec = (carve(TILES) for _ in range(9))
        tiles_e, tin, tex = carve(E), carve(E), carve(E)
        pos_j = carve(TOPK * TILES)
        pos_i, tile_i, slot_i = (carve(TOPK * TILES).bitcast(I32) for _ in range(3))
        tile_f, slot_f = carve(TOPK * TILES), carve(TOPK * TILES)
        RG = 8
        is_slot = [carve(RG * P).rearrange("p (g s) -> p g s", g=RG) for _ in range(2)]
        is_tile = [carve(RG * UNITS).rearrange("p (g s) -> p g s", g=RG) for _ in range(2)]
        tile_val = [carve(RG * UNITS).rearrange("p (g s) -> p g s", g=RG) for _ in range(2)]
        ecmp = carve(SLOT_TILES * (E - 1)).rearrange("p (k e) -> p k e", e=E - 1)
        ecount = carve(SLOT_TILES)
        pad_p, dest_f, wrap1, wrap2, tok_f = (carve(UNITS) for _ in range(5))

        at[0] = 0
        xg = [carve(SUBS * D).rearrange("p (u n) -> p u n", u=SUBS) for _ in range(2)]
        xt_hi, xt_lo = ([carve(HC * SLOTS, F16).rearrange("p (c n) -> p c n", c=HC) for _ in range(2)] for _ in range(2))
        GQ = 4
        g_s = [carve(512) for _ in range(GQ)]
        g_hi, g_lo = ([carve(IC * SLOTS, F16).rearrange("p (c n) -> p c n", c=IC) for _ in range(2)] for _ in range(2))
        y_s = [carve(SUBS * D) for _ in range(2)]
        gidx, didx = ([carve(SUBS).bitcast(I32) for _ in range(2)] for _ in range(2))

        at[0] = 0
        CG = 2
        GROUPS = TILES // CG
        y_in = [carve(TOPK * CG * D).rearrange("p (j g n) -> p j g n", j=TOPK, g=CG) for _ in range(2)]
        f_s = [carve(CG * D).rearrange("p (g n) -> p g n", g=CG) for _ in range(2)]
        o_s = [carve(CG * D).rearrange("p (g n) -> p g n", g=CG) for _ in range(2)]
        c_st = [carve(CG * 6).rearrange("p (g n) -> p g n", g=CG) for _ in range(2)]
        c_mv = [carve(CG * 2).rearrange("p (g n) -> p g n", g=CG) for _ in range(2)]
        c_ve = carve(CG)
        c_rs = [carve(CG) for _ in range(2)]
        neg_half, eps = sb("neg_half", [P, CG]), sb("eps", [P, CG])

        ps_a = es.enter_context(nc.psum_tensor("ps_a", [P, 4, 512], F32))
        ps_b = es.enter_context(nc.psum_tensor("ps_b", [P, 2, 512], F32))
        ps_c = es.enter_context(nc.psum_tensor("ps_c", [P, 2, 512], F32))
        ps_s = ps_a[:, 0:2, :].rearrange("p a (x s k) -> p (a x) s k", s=STRIPS, k=BLOCK)
        half_bank = lambda m, h: ps_c[:, m, h * 256:(h + 1) * 256].rearrange("p (c n) -> p c n", c=HC)
        ps_xt = ps_v = ps_ot = half_bank(0, 0)
        ps_x2t = half_bank(0, 1)
        ps_q, ps_k, ps_wo = half_bank(1, 0), half_bank(1, 1), half_bank(1, 0)
        ps_pt = ps_b[:, :, :].rearrange("p a (h n) -> p (a h) n", n=P)
        ps_o = ps_b[:, :, 0:4 * NB * VCOLS].rearrange("p a (y x) -> p a y x", x=VCOLS)
        ps_lg = ps_c[:, 1, 256:256 + E]
        ps_h = ps_a
        ps_y = ps_b
        ps_x = ps_c

        loaded = sem("loaded")
        x_in = [sem(f"x_in{i}") for i in range(2)]
        ctx_in = [sem(f"ctx_in{i}") for i in range(2)]
        w_in = [sem(f"w_in{i}") for i in range(2)]
        xn2_out = [sem(f"xn2_out{i}") for i in range(2)]
        zeroed = sem("zeroed")
        st1, mv1_r, ve1_r, rs1_r, xn_r = (sem(n) for n in ("st1", "mv1_r", "ve1_r", "rs1_r", "xn_r"))
        st2, mv2_r, ve2_r, rs2_r, xn2_r = (sem(n) for n in ("st2", "mv2_r", "ve2_r", "rs2_r", "xn2_r"))
        bo_added, x1_r, xn2_added = sem("bo_added"), sem("x1_r"), sem("xn2_added")
        xt_ps, xt_r = sem("xt_ps"), sem("xt_r")
        q_r, qb_r, k_ps, k_r, v_ps, v_r = (sem(n) for n in ("q_r", "qb_r", "k_ps", "k_r", "v_ps", "v_r"))
        s_ps, max_r, sub_r, p_r, pt_ps, pt_r = (sem(n) for n in ("s_ps", "max_r", "sub_r", "p_r", "pt_ps", "pt_r"))
        o_ps, osum_r, o_r, ot_ps, ot_r, wo_ps = (sem(n) for n in ("o_ps", "osum_r", "o_r", "ot_ps", "ot_r", "wo_ps"))
        x2t_ps, x2t_r, lg_ps, lg_r = (sem(n) for n in ("x2t_ps", "x2t_r", "lg_ps", "lg_r"))
        w_scaled, w_hi_r, w_lo_r = sem("w_scaled"), sem("w_hi_r"), sem("w_lo_r")

        def here(j, u, skew):
            return 2 * j + (u + skew), j + (u + skew) // 2, (u + skew) % 2

        def flat2(v):
            return v.rearrange("p c n -> p (c n)")

        def valid(t):
            return not isinstance(t, int) or 0 <= t < TILES

        FIRST, LAST = 6, TILES - 4

        def steps(eng, lo, step):
            for i in range(lo, FIRST):
                step(i // 2, i % 2)
            with eng.Fori(FIRST // 2, LAST // 2) as j:
                step(j, 0)
                step(j, 1)
            for i in range(LAST, TILES + 5):
                step(i // 2, i % 2)

        def since(eng, s, count):
            if not isinstance(count, int) or count > 0:
                eng.wait_ge(s, count)

        passed = {n: sem(f"passed_{n}") for n in ("dve", "pool")}

        def settled(eng):
            eng.sem_inc(passed["dve" if eng.engine == nc.vector.engine else "pool"], 1)

        block = es.enter_context(nc.Block())

        small = [(cst[:, :], consts), (wq_s, wq), (wk_s, wk), (wv_s, wv), (wo_s, wo), (bq_s, bq), (bk_s, bk), (bv_s, bv),
                 (bo_s, bo), (gate_w[:, :, :], gate_t), (gate_bias[:, :], gate_b)]
        ALL_LOADED = 16 * len(small)

        rt = sem("rt")
        rt_shifted, rt_exp, rt_mask = sem("rt_shifted"), sem("rt_exp"), sem("rt_mask")
        rt_cnt = sem("rt_cnt")
        rt_slot = sem("rt_slot")
        rt_grp = sem("rt_grp")
        rt_grp_used = sem("rt_grp_used")
        rt_unit = sem("rt_unit")
        routed = sem("routed")
        gat = [sem(f"gat{i}") for i in range(2)]
        scat = [sem(f"scat{i}") for i in range(2)]
        gidx_r, didx_r = sem("gidx_r"), sem("didx_r")
        gt_ps, xh_r, xl_r, h_ps, g_r, gh_r, gl_r, y_ps, y_r = (
            sem(n) for n in ("gt_ps", "xh_r", "xl_r", "h_ps", "g_r", "gh_r", "gl_r", "y_ps", "y_r"))
        rc_in = sem("rc_in")
        power_r = sem("power_r")
        yin = [sem(f"yin{i}") for i in range(2)]
        outs = [sem(f"outs{i}") for i in range(2)]
        c_f0, c_f1, c_stats, c_mvr, c_ver, c_rsr, c_ap, c_out = (
            sem(n) for n in ("c_f0", "c_f1", "c_stats", "c_mvr", "c_ver", "c_rsr", "c_ap", "c_out"))

        MOE_FIRST, MOE_LAST = 4, 36

        def moe_steps(eng, lo, step):
            for k in range(lo, MOE_FIRST):
                step(k // 2, k % 2)
            with eng.Fori(MOE_FIRST // 2, MOE_LAST // 2) as j:
                step(j, 0)
                step(j, 1)
            for k in range(MOE_LAST, SLOT_TILES + 1):
                step(k // 2, k % 2)

        def moe_valid(k):
            return not isinstance(k, int) or 0 <= k < SLOT_TILES

        def group_steps(eng, lo, hi, step):
            for g in range(lo, 4):
                step(g // 2, g % 2)
            with eng.Fori(2, GROUPS // 2) as j:
                step(j, 0)
                step(j, 1)
            for g in range(GROUPS, hi):
                step(g // 2, g % 2)

        def group_valid(g):
            return not isinstance(g, int) or 0 <= g < GROUPS

        @block.sync
        def _(sp):
            def step(j, u):
                t, half, b = here(j, u, 3)
                if valid(t):
                    since(sp, x_in[b], 16 * half)
                    sp.dma_start(resid[:, bass.ds(t, 1), :], x[bass.ds(t, 1)].rearrange("a p d -> p a d")).then_inc(x_in[b], 16)
                t, half, b = here(j, u, 1)
                if valid(t):
                    since(sp, v_ps, t - 1)
                    sp.dma_start(ctx[b], ctx_t[bass.ds(t, 1)].rearrange("a p c n -> p (a c) n")).then_inc(ctx_in[b], 16)
                t, half, b = here(j, u, 0)
                if valid(t):
                    since(sp, w_lo_r, t - 1)
                    sp.dma_start(staging[b], weights[bass.ds(t, 1)].rearrange("a p n -> p (a n)")).then_inc(w_in[b], 16)
                t, half, b = here(j, u, -3)
                if valid(t):
                    sp.wait_ge(xn2_r, t + 1)
                    sp.dma_start(xn_rows[bass.ds(t * P, P), :], xn2).then_inc(xn2_out[b], 16)
            for i in range(-3, 0):
                step(i // 2, i % 2)
            steps(sp, 0, step)
            for b in range(2):
                sp.wait_ge(xn2_out[b], 16 * TILES // 2)
            sp.wait_ge(wo_ps, TILES)
            sp.wait_ge(bo_added, TILES)
            sp.dma_start(rc, route_consts).then_inc(rc_in, 16)

            sp.wait_ge(scat[0], 16 * SUBS * ((SLOT_TILES + 1) // 2))
            sp.wait_ge(scat[1], 16 * SUBS * (SLOT_TILES // 2))
            y_two = y_rows[0:TOPK * TOKENS, :].rearrange("(j g t p) d -> g j p t d", j=TOPK, t=CG, p=P)
            out_g = out.rearrange("(g t) p d -> g p t d", t=CG)

            def group(j, u):
                g, half, b = here(j, u, 0)
                if group_valid(g):
                    since(sp, c_f1, CG * (g - 1))
                    for c in range(TOPK):
                        sp.dma_start(y_in[b][:, c], y_two[bass.ds(g, 1), c].rearrange("a p t d -> p (a t) d")).then_inc(yin[b], 16)
                g, half, b = here(j, u, -2)
                if group_valid(g):
                    sp.wait_ge(c_out, g + 1)
                    sp.dma_start(out_g[bass.ds(g, 1)].rearrange("a p t d -> p (a t) d"), o_s[b]).then_inc(outs[b], 16)
            group_steps(sp, 0, GROUPS + 2, group)
            for b in range(2):
                sp.wait_ge(outs[b], 16 * GROUPS // 2)

        @block.tensor
        def _(pe):
            pe.wait_ge(loaded, ALL_LOADED)
            pe.wait_ge(zeroed, 4)

            def step(j, u):
                t, half, b = here(j, u, 1)
                if valid(t):
                    pe.wait_ge(xn_r, t + 1)
                    since(pe, ot_r, 2 * (t - 3))
                    since(pe, x2t_r, t - 4)
                    since(pe, v_r, 2 * (t - 1))
                    for c in range(HC):
                        mm = pe.transpose(ps_xt[:, c, :], xn[:, c * P:(c + 1) * P], ident)
                    mm.then_inc(xt_ps, 1)
                t, half, b = here(j, u, 0)
                if valid(t):
                    pe.wait_ge(q_r, t + 1)
                    pe.wait_ge(k_r, STRIPS * (t + 1))
                    since(pe, sub_r, t)
                    for c in range(HC):
                        for n in range(NB):
                            mm = pe.matmul(ps_s[:, c * NB + n, :, :].rearrange("p s k -> p (s k)"),
                                           q_m[:, c, n].rearrange("p h q -> p (h q)"),
                                           k_bd[:, c, n].rearrange("p s k -> p (s k)"), start=True, stop=True)
                    mm.then_inc(s_ps, 1)
                t, half, b = here(j, u, -1)
                if valid(t):
                    pe.wait_ge(p_r, t + 1)
                    since(pe, o_r, 4 * t)
                    for h in range(PAIRS):
                        mm = pe.transpose(ps_pt[:, h, :], prob[:, h * P:(h + 1) * P], ident)
                    mm.then_inc(pt_ps, 1)
                t, half, b = here(j, u, 1)
                if valid(t):
                    pe.wait_ge(xt_r, t + 1)
                    since(pe, x1_r, t - 3)
                    since(pe, lg_r, t - 4)
                    for c in range(HC):
                        for k in range(HC):
                            mm = pe.matmul(ps_q[:, c, :], wq_s[:, k, c * P:(c + 1) * P], xn_t[:, k, :],
                                           start=(k == 0), stop=(k == HC - 1))
                    pe.wait_ge(ctx_in[b], 16 * (half + 1))
                    for c in range(HC):
                        for k in range(HC):
                            mm = pe.matmul(ps_k[:, c, :], wk_s[:, k, c * P:(c + 1) * P], ctx[b][:, k, :],
                                           start=(k == 0), stop=(k == HC - 1))
                    mm.then_inc(k_ps, 1)
                t, half, b = here(j, u, 0)
                if valid(t):
                    pe.wait_ge(ctx_in[b], 16 * (half + 1))
                    if valid(t + 1):
                        pe.wait_ge(xt_r, t + 2)
                    for k in range(HC):
                        mm = pe.matmul(flat2(ps_v), ctx[b][:, k, :], wv_s[:, k, :], start=(k == 0), stop=(k == HC - 1))
                    mm.then_inc(v_ps, 1)
                t, half, b = here(j, u, -1)
                if valid(t):
                    pe.wait_ge(pt_r, t + 1)
                    pe.wait_ge(v_r, 2 * (t + 1))
                    for h in range(PAIRS):
                        mm = pe.matmul(ps_o[:, h // 4, (h % 4) * NB:(h % 4 + 1) * NB, :], prob_t[:, h, :],
                                       v_x[b][:, h // HC, h % HC, :, :], start=True, stop=True)
                    mm.then_inc(o_ps, 1)
                t, half, b = here(j, u, -2)
                if valid(t):
                    pe.wait_ge(o_r, 4 * (t + 1))
                    if valid(t + 2):
                        pe.wait_ge(v_r, 2 * (t + 3))
                    for n in range(NB):
                        mm = pe.transpose(ps_ot[:, n, :], o_n[:, n, :], ident)
                    mm.then_inc(ot_ps, 1)
                t, half, b = here(j, u, -3)
                if valid(t):
                    pe.wait_ge(xn2_r, t + 1)
                    since(pe, x2t_r, t)
                    for c in range(HC):
                        mm = pe.transpose(ps_x2t[:, c, :], xn2[:, c * P:(c + 1) * P], ident)
                    mm.then_inc(x2t_ps, 1)
                t, half, b = here(j, u, -2)
                if valid(t):
                    pe.wait_ge(ot_r, 2 * (t + 1))
                    if valid(t + 3):
                        pe.wait_ge(k_r, STRIPS * (t + 4))
                    since(pe, x1_r, t)
                    since(pe, lg_r, t - 1)
                    for h in range(2):
                        mm = pe.matmul(flat2(ps_wo), o_t[:, h, :], wo_s[:, h, :], start=(h == 0), stop=(h == 1))
                    mm.then_inc(wo_ps, 1)
                t, half, b = here(j, u, -3)
                if valid(t):
                    pe.wait_ge(x2t_r, t + 1)
                    pe.wait_ge(x1_r, t + 1)
                    since(pe, lg_r, t)
                    for k in range(HC):
                        mm = pe.matmul(ps_lg, xn2_t[:, k, :], gate_w[:, k, :], start=(k == 0), stop=(k == HC - 1))
                    mm.then_inc(lg_ps, 1)
            step(-1, 1)
            steps(pe, 0, step)

            pe.wait_ge(rt_mask, 1)
            pe.wait_ge(rc_in, 16)
            pe.matmul(ps_b[:, 0, 0:E * TILES], rc[:, R_TRI:R_TRI + P], mk.rearrange("p e t -> p (e t)"), start=True, stop=True)
            pe.matmul(ps_b[:, 1, 0:E * TILES], rc[:, R_ONES:R_ONES + P], mk.rearrange("p e t -> p (e t)"),
                      start=True, stop=True).then_inc(rt_cnt, 1)
            for g in range(TOPK * TILES):
                if g % RG == 0:
                    pe.wait_ge(rt_grp, g // RG + 1)
                    pe.wait_ge(rt_slot, g // RG + 1)
                mm = pe.matmul(ps_c[:, 0, 0:UNITS], is_slot[g // RG % 2][:, g % RG, :], tile_val[g // RG % 2][:, g % RG, :],
                               start=(g == 0), stop=(g == TOPK * TILES - 1))
                if g % RG == RG - 1:
                    mm.then_inc(rt_grp_used, 1)

            pe.wait_ge(routed, 1)
            pe.wait_ge(w_lo_r, WSTEPS)

            def transpose_rows(k, half, b):
                pe.wait_ge(gat[b], 16 * SUBS * (half + 1))
                since(pe, xl_r, k - 1)
                for c in range(HC):
                    for v in range(SUBS):
                        at = c * SLOTS + v * P
                        mm = pe.transpose(ps_x[:, b, at:at + P], xg[b][:, v, c * P:(c + 1) * P], ident)
                mm.then_inc(gt_ps, 1)

            def expert_of(k):
                e = pe.value_load(slot_expert[0:1, bass.ds(k, 1)], min_val=0, max_val=E - 1)
                return pe.snap(e * (2 * EXPERT_COLS))

            def up(k, b, first):
                pe.wait_ge(xl_r, k + 1)
                for ic in range(IC):
                    q = ic // 2
                    if ic % 2 == 0:
                        since(pe, g_r, GQ * (k - 1) + q + 1)
                    n = 0
                    for hc in range(HC):
                        for w, r in ((w_hi, xt_hi), (w_hi, xt_lo), (w_lo, xt_hi)):
                            mm = pe.matmul(ps_h[:, q, (ic % 2) * SLOTS:(ic % 2 + 1) * SLOTS],
                                           w[:, bass.ds(first + (hc * I + ic * P), P)], r[b][:, hc, :],
                                           start=(n == 0), stop=(n == 3 * HC - 1))
                            n += 1
                    if ic % 2:
                        mm.then_inc(h_ps, 1)

            def down(k, b, first):
                since(pe, y_r, k - 1)
                pe.wait_ge(gl_r, GQ * (k + 1))
                for v in range(SUBS):
                    n = 0
                    for ic in range(IC):
                        for g, w in ((g_hi, w_hi), (g_lo, w_hi), (g_hi, w_lo)):
                            mm = pe.matmul(ps_y[:, b, v * D:(v + 1) * D], g[b][:, ic, v * P:(v + 1) * P],
                                           w[:, bass.ds(first + (EXPERT_COLS + ic * D), D)],
                                           start=(n == 0), stop=(n == 3 * IC - 1))
                            n += 1
                mm.then_inc(y_ps, 1)

            def moe(j, u):
                k, half, b = here(j, u, 2)
                if moe_valid(k):
                    transpose_rows(k, half, b)
                k, half, b = here(j, u, 1)
                if moe_valid(k):
                    up(k, b, expert_of(k))
                k, half, b = here(j, u, 0)
                if moe_valid(k):
                    down(k, b, expert_of(k))
            moe(-1, 0)
            moe(-1, 1)
            moe_steps(pe, 0, moe)

        @block.vector
        def _(dve):
            dve.memset(v_x[0], 0.0).then_inc(zeroed, 1)
            dve.memset(v_x[1], 0.0).then_inc(zeroed, 1)
            dve.memset(k_bd.rearrange("p c b s k -> p (c b s k)"), 0.0).then_inc(zeroed, 1)
            dve.wait_ge(zeroed, 3)
            for b in range(2):
                for n in range(NB):
                    r = slice(n * BLOCK, (n + 1) * BLOCK)
                    ins = dve.memset(v_x[b][r, :, :, n, 2 * DK:VCOLS].rearrange("p s c x -> p (s c) x"), 1.0)
            ins.then_inc(zeroed, 1)

            def step(j, u):
                t, half, b = here(j, u, -3)
                if valid(t):
                    dve.wait_ge(wo_ps, t + 1)
                    since(dve, lg_ps, t)
                    dve.wait_ge(bo_added, t + 1)
                    r = resid[:, bass.ds(t, 1), :].rearrange("p a d -> p (a d)")
                    dve.tensor_tensor(r, ps_wo.rearrange("p c n -> p (c n)"), r, ALU.add).then_inc(x1_r, 1)
                    since(dve, mv2_r, t)
                    dve.wait_ge(x1_r, t + 1)
                    settled(dve)
                    dve.bn_stats(stats2, r).then_inc(st2, 1)
                    since(dve, ve2_r, t - 1)
                    since(dve, xn2_r, t - 1)
                    dve.wait_ge(st2, t + 1)
                    settled(dve)
                    dve.bn_aggr(mv2[b], stats2).then_inc(mv2_r, 1)
                t, half, b = here(j, u, -4)
                if valid(t):
                    dve.wait_ge(lg_ps, t + 1)
                    dve.tensor_tensor(logits[:, :, bass.ds(t, 1)], ps_lg.unsqueeze(2), gate_bias[:, :].unsqueeze(2), ALU.add).then_inc(lg_r, 1)
                t, half, b = here(j, u, 0)
                if valid(t):
                    since(dve, sub_r, t)
                    dve.wait_ge(s_ps, t + 1)
                    dve.tensor_reduce(row_max.rearrange("p (x s) -> p x s", s=STRIPS), ps_s, AX.X, ALU.max).then_inc(max_r, 1)
                t, half, b = here(j, u, 3)
                if valid(t):
                    since(dve, mv1_r, t)
                    dve.wait_ge(x_in[b], 16 * (half + 1))
                    settled(dve)
                    dve.bn_stats(stats1, resid[:, bass.ds(t, 1), :].rearrange("p a d -> p (a d)")).then_inc(st1, 1)
                    since(dve, ve1_r, t - 1)
                    since(dve, xn_r, t - 1)
                    dve.wait_ge(st1, t + 1)
                    settled(dve)
                    dve.bn_aggr(mv1[b], stats1).then_inc(mv1_r, 1)
                t, half, b = here(j, u, 0)
                if valid(t):
                    dve.wait_ge(max_r, t + 1)
                    since(dve, pt_ps, t)
                    dve.tensor_tensor(prob.rearrange("p (s x k) -> p x s k", s=STRIPS, k=BLOCK), ps_s,
                                      row_max.rearrange("p (x s) -> p x s", s=STRIPS).unsqueeze(3).to_broadcast([P, HC * NB, STRIPS, BLOCK]),
                                      ALU.subtract).then_inc(sub_r, 1)
                t, half, b = here(j, u, -3)
                if valid(t):
                    dve.wait_ge(rs2_r, t + 1)
                    since(dve, xn2_out[1 - b], 16 * (half + b))
                    since(dve, x2t_ps, t)
                    since(dve, xn2_added, t)
                    dve.tensor_scalar(xn2, resid[:, bass.ds(t, 1), :].rearrange("p a d -> p (a d)"), mv2[b][:, 0:1], rs2[b],
                                      ALU.subtract, ALU.mult).then_inc(xn2_r, 1)
                t, half, b = here(j, u, 1)
                if valid(t):
                    dve.wait_ge(k_ps, t + 1)
                    since(dve, q_r, t)
                    dve.tensor_tensor(q_b, ps_q, bq_s.unsqueeze(2).to_broadcast([P, HC, P]), ALU.add).then_inc(qb_r, 1)
                    for s in range(STRIPS):
                        r = slice(32 * s, 32 * s + 32)
                        dve.tensor_tensor(k_bd[r, :, :, s, :], ps_k[r].rearrange("p c (b k) -> p c b k", b=NB),
                                          bk_s[r].unsqueeze(2).unsqueeze(3).to_broadcast([32, HC, NB, BLOCK]), ALU.add).then_inc(k_r, 1)
                t, half, b = here(j, u, 2)
                if valid(t):
                    dve.wait_ge(rs1_r, t + 1)
                    since(dve, xt_ps, t)
                    dve.tensor_scalar(xn, resid[:, bass.ds(t, 1), :].rearrange("p a d -> p (a d)"), mv1[b][:, 0:1], rs1[b],
                                      ALU.subtract, ALU.mult).then_inc(xn_r, 1)
                t, half, b = here(j, u, -1)
                if valid(t):
                    dve.wait_ge(o_ps, t + 1)
                    since(dve, ot_ps, t)
                    since(dve, o_r, 4 * t)
                    dve.reciprocal(o_sum.rearrange("p (a y) -> p a y", a=2), ps_o[:, :, :, 2 * DK]).then_inc(osum_r, 1)
                    dve.wait_ge(osum_r, t + 1)
                    for h in range(2):
                        r = slice(h * BLOCK, (h + 1) * BLOCK)
                        for m in range(NB):
                            dve.tensor_tensor(o_n[r, m, :].rearrange("p (a y d) -> p a y d", a=2, d=DK),
                                              ps_o[r].rearrange("p a (y b) x -> p a y b x", b=NB)[:, :, :, m, h * DK:(h + 1) * DK],
                                              o_sum[r].rearrange("p (a y b) -> p a y b", a=2, b=NB)[:, :, :, m:m + 1].to_broadcast([BLOCK, 2, 4, DK]),
                                              ALU.mult).then_inc(o_r, 1)
            for i in range(-3, -1):
                step(i // 2, i % 2)
            dve.wait_ge(loaded, ALL_LOADED)
            step(-1, 1)
            steps(dve, 0, step)

            n = [0]

            def link(ins):
                n[0] += 1
                ins.then_inc(rt, 1)
                dve.wait_ge(rt, n[0])

            def over_e(v):
                return v.rearrange("p e t -> p t e")

            def per_t(v):
                return v.unsqueeze(1).to_broadcast([P, E, TILES])

            dve.wait_ge(lg_r, TILES)
            dve.wait_ge(ot_r, 2 * TILES)
            dve.wait_ge(x2t_r, TILES)
            dve.wait_ge(xn2_added, TILES)
            dve.wait_ge(w_lo_r, WSTEPS)
            dve.wait_ge(wo_ps, TILES)
            for b in range(2):
                dve.wait_ge(xn2_out[b], 16 * TILES // 2)
            dve.wait_ge(rc_in, 16)
            desc = rc[:, R_DESC:R_DESC + E * TILES].rearrange("p (e t) -> p e t", e=E)
            link(dve.memset(keep, 1.0))
            link(dve.memset(keep[:, :, 0:1], 0.0))
            link(dve.tensor_reduce(lmax, over_e(logits[:, :, :]), AX.X, ALU.max))
            dve.tensor_tensor(lg_s, logits[:, :, :], per_t(lmax), ALU.subtract).then_inc(rt_shifted, 1)
            dve.wait_ge(rt_exp, 1)
            link(dve.tensor_reduce(lsum, over_e(ex), AX.X, ALU.add))
            link(dve.reciprocal(lrec, lsum))
            link(dve.tensor_tensor(ex, ex, per_t(lrec), ALU.mult))
            for m, i, oh in ((m1, i1, oh1), (m2, i2, oh2)):
                link(dve.tensor_reduce(m, over_e(ex), AX.X, ALU.max))
                link(dve.tensor_tensor(eq, ex, per_t(m), ALU.is_equal))
                link(dve.tensor_tensor(eq, eq, desc, ALU.mult))
                link(dve.tensor_reduce(i, over_e(eq), AX.X, ALU.max))
                link(dve.tensor_tensor(oh, desc, per_t(i), ALU.is_equal))
                if m is m1:
                    link(dve.scalar_tensor_tensor(ex, oh, -4.0, ex, ALU.mult, ALU.add))
            dve.tensor_tensor(mk, oh1, oh2, ALU.add).then_inc(rt_mask, 1)
            link(dve.scalar_tensor_tensor(den, m1, GATE_EPS, m2, ALU.add, ALU.add))
            link(dve.reciprocal(drec, den))
            link(dve.tensor_tensor(mix_w[:, 0, :], m1, drec, ALU.mult))
            link(dve.tensor_tensor(mix_w[:, 1, :], m2, drec, ALU.mult))
            dve.wait_ge(rt_cnt, 1)
            flat = lambda v: v.rearrange("p e t -> p (e t)")
            link(dve.tensor_copy(flat(tot), ps_b[:, 1, 0:E * TILES]))
            link(dve.tensor_tensor_scan(flat(incl), flat(keep), flat(tot), 0.0, ALU.mult, ALU.add))
            link(dve.tensor_tensor(base, incl, tot, ALU.subtract))
            first_slots = rc[:, R_STEP:R_STEP + TILES]
            link(dve.tensor_tensor(eq, incl[:, :, TILES - 1:TILES].to_broadcast([P, E, TILES]), per_t(first_slots), ALU.is_gt))
            link(dve.tensor_reduce(tiles_e, eq, AX.X, ALU.add))
            link(dve.tensor_tensor_scan(tin, rc[:, R_ONES:R_ONES + E], tiles_e, 0.0, ALU.mult, ALU.add))
            link(dve.tensor_tensor(tex, tin, tiles_e, ALU.subtract))
            link(dve.scalar_tensor_tensor(base, tex.unsqueeze(2).to_broadcast([P, E, TILES]), float(SLOTS), base, ALU.mult, ALU.add))
            link(dve.tensor_tensor(flat(pos), ps_b[:, 0, 0:E * TILES], flat(base), ALU.add))
            for c, oh in ((0, oh1), (1, oh2)):
                link(dve.tensor_tensor(eq, oh, pos, ALU.mult))
                link(dve.tensor_reduce(pos_j[:, c * TILES:(c + 1) * TILES], over_e(eq), AX.X, ALU.add))
            link(dve.tensor_copy(pos_i, pos_j))
            link(dve.tensor_scalar(tile_i, pos_i, P.bit_length() - 1, None, ALU.arith_shift_right))
            link(dve.tensor_scalar(slot_i, pos_i, P - 1, None, ALU.bitwise_and))
            link(dve.tensor_copy(tile_f, tile_i))
            link(dve.tensor_copy(slot_f, slot_i))
            for c in range(TOPK * TILES // RG):
                g = slice(c * RG, (c + 1) * RG)
                if c >= 2:
                    dve.wait_ge(rt_grp, c - 1)
                dve.tensor_tensor(is_tile[c % 2], rc[:, R_IOTA:R_IOTA + UNITS].unsqueeze(1).to_broadcast([P, RG, UNITS]),
                                  tile_f[:, g].unsqueeze(2).to_broadcast([P, RG, UNITS]), ALU.is_equal).then_inc(rt_unit, 1)
                if c >= 2:
                    dve.wait_ge(rt_grp_used, c - 1)
                dve.tensor_tensor(is_slot[c % 2], rc[:, R_IOTA:R_IOTA + P].unsqueeze(1).to_broadcast([P, RG, P]),
                                  slot_f[:, g].unsqueeze(2).to_broadcast([P, RG, P]), ALU.is_equal).then_inc(rt_slot, 1)
            link(dve.tensor_tensor(ecmp, tex[:, 1:E].unsqueeze(1).to_broadcast([P, SLOT_TILES, E - 1]),
                                   rc[:, R_IOTA:R_IOTA + SLOT_TILES].unsqueeze(2).to_broadcast([P, SLOT_TILES, E - 1]), ALU.is_le))
            link(dve.tensor_reduce(ecount, ecmp, AX.X, ALU.add))
            link(dve.tensor_copy(slot_expert[:, :], ecount))
            dve.wait_ge(rt_grp_used, TOPK * TILES // RG)
            ps_slot = ps_c[:, 0, 0:UNITS]
            link(dve.scalar_tensor_tensor(pad_p, ps_slot, 0.0, rc[:, R_PAD:R_PAD + UNITS], ALU.is_ge, ALU.mult))
            link(dve.scalar_tensor_tensor(dest_f, ps_slot, float(TOPK * TOKENS), pad_p, ALU.add, ALU.add))
            link(dve.tensor_copy(slot_dest[:, :], dest_f))
            link(dve.tensor_scalar(wrap1, dest_f, float(TOKENS), -float(TOKENS), ALU.is_ge, ALU.mult))
            link(dve.tensor_scalar(wrap2, dest_f, float(TOPK * TOKENS), -float(TOKENS), ALU.is_ge, ALU.mult))
            link(dve.tensor_tensor(tok_f, dest_f, wrap1, ALU.add))
            link(dve.tensor_tensor(tok_f, tok_f, wrap2, ALU.add))
            dve.tensor_copy(slot_token[:, :], tok_f).then_inc(routed, 1)

            dve.wait_ge(routed, 1)

            def moe(j, u):
                k, half, b = here(j, u, 2)
                if moe_valid(k):
                    dve.wait_ge(gt_ps, k + 1)
                    since(dve, h_ps, GQ * (k - 1))
                    src = ps_x[:, b, :].rearrange("p (c n) -> p c n", c=HC)
                    dve.tensor_scalar(xt_hi[b], src, X_SCALE, None, ALU.mult).then_inc(xh_r, 1)
                    dve.wait_ge(xh_r, k + 1)
                    dve.scalar_tensor_tensor(xt_lo[b], src, X_SCALE, xt_hi[b], ALU.mult, ALU.subtract).then_inc(xl_r, 1)
                k, half, b = here(j, u, 1)
                if moe_valid(k):
                    since(dve, y_ps, k - 1)
                    for q in range(GQ):
                        c = slice(q * IC // GQ, (q + 1) * IC // GQ)
                        src = g_s[q].rearrange("p (c n) -> p c n", n=SLOTS)
                        dve.wait_ge(g_r, GQ * k + 1 + q)
                        dve.tensor_scalar(g_hi[b][:, c, :], src, G_SCALE, None, ALU.mult).then_inc(gh_r, 1)
                        dve.wait_ge(gh_r, GQ * k + 1 + q)
                        dve.scalar_tensor_tensor(g_lo[b][:, c, :], src, G_SCALE, g_hi[b][:, c, :], ALU.mult, ALU.subtract).then_inc(gl_r, 1)
            moe(-1, 0)
            moe(-1, 1)
            moe_steps(dve, 0, moe)

            def group(j, u):
                g, half, b = here(j, u, 0)
                if group_valid(g):
                    for r in range(CG):
                        dve.wait_ge(c_f0, CG * g + r + 1)
                        dve.scalar_tensor_tensor(f_s[b][:, r, :], y_in[b][:, 1, r, :], mix_w[:, 1, bass.ds(CG * g + r, 1)],
                                                 f_s[b][:, r, :], ALU.mult, ALU.add).then_inc(c_f1, 1)
                    for r in range(CG):
                        since(dve, c_mvr, CG * (g - 2) + r + 1)
                        dve.wait_ge(c_f1, CG * g + r + 1)
                        settled(dve)
                        dve.bn_stats(c_st[b][:, r, :], f_s[b][:, r, :]).then_inc(c_stats, 1)
                g, half, b = here(j, u, -1)
                if group_valid(g):
                    for r in range(CG):
                        dve.wait_ge(c_rsr, g + 1)
                        dve.tensor_scalar(f_s[b][:, r, :], f_s[b][:, r, :], c_mv[b][:, r, 0:1], c_rs[b][:, r:r + 1],
                                          ALU.subtract, ALU.mult).then_inc(c_ap, 1)
                g, half, b = here(j, u, 0)
                if group_valid(g):
                    since(dve, c_ap, CG * (g - 1))
                    for r in range(CG):
                        dve.wait_ge(c_stats, CG * g + r + 1)
                        settled(dve)
                        dve.bn_aggr(c_mv[b][:, r, :], c_st[b][:, r, :]).then_inc(c_mvr, 1)
            group_steps(dve, 0, GROUPS + 1, group)

        @block.scalar
        def _(act):
            for dst, src in small:
                act.dma_start(dst, src).then_inc(loaded, 16)
            act.wait_ge(loaded, ALL_LOADED)
            act.wait_ge(zeroed, 4)

            def step(j, u):
                t, half, b = here(j, u, 1)
                if valid(t):
                    act.wait_ge(xt_ps, t + 1)
                    since(act, k_ps, t)
                    since(act, lg_ps, t - 4)
                    act.activation(xn_t, ps_xt, ACT.Copy).then_inc(xt_r, 1)
                t, half, b = here(j, u, 0)
                if valid(t):
                    act.wait_ge(w_in[b], 16 * (half + 1))
                    act.activation(staging[b], staging[b], ACT.Copy, scale=W_SCALE).then_inc(w_scaled, 1)
                t, half, b = here(j, u, -1)
                if valid(t):
                    act.wait_ge(w_scaled, t + 1)
                    act.activation(w_hi[:, bass.ds(t * WCOLS, WCOLS)], staging[b], ACT.Copy).then_inc(w_hi_r, 1)
                t, half, b = here(j, u, -1)
                if valid(t):
                    act.wait_ge(pt_ps, t + 1)
                    since(act, o_ps, t)
                    act.activation(prob_t, ps_pt, ACT.Copy).then_inc(pt_r, 1)
                t, half, b = here(j, u, 0)
                if valid(t):
                    act.wait_ge(v_ps, t + 1)
                    since(act, o_ps, t - 1)
                    for n in range(NB):
                        r = slice(n * BLOCK, (n + 1) * BLOCK)
                        act.activation(v_x[b][r, :, :, n, 0:2 * DK],
                                       ps_v[r].rearrange("p c (s d) -> p s c d", s=STRIPS), ACT.Copy).then_inc(v_r, 1)
                    act.wait_ge(sub_r, t + 1)
                    act.activation(prob, prob, ACT.Exp, scale=DK ** -0.5).then_inc(p_r, 1)
                t, half, b = here(j, u, -2)
                if valid(t):
                    act.wait_ge(ot_ps, t + 1)
                    since(act, x2t_ps, t)
                    since(act, wo_ps, t)
                    for h in range(2):
                        act.activation(o_t[:, h, :].rearrange("p (b q) -> p b q", b=NB), ps_ot[:, :, h * BLOCK:(h + 1) * BLOCK],
                                       ACT.Identity, bias=bv_s[:, h:h + 1]).then_inc(ot_r, 1)
                t, half, b = here(j, u, -3)
                if valid(t):
                    act.wait_ge(x2t_ps, t + 1)
                    since(act, lg_ps, t)
                    act.activation(xn2_t, ps_x2t, ACT.Copy).then_inc(x2t_r, 1)
            step(-1, 1)
            steps(act, 0, step)

            act.wait_ge(rt_shifted, 1)
            act.activation(ex, lg_s, ACT.Exp).then_inc(rt_exp, 1)
            act.wait_ge(routed, 1)

            def moe(j, u):
                k, half, b = here(j, u, 1)
                if moe_valid(k):
                    for q in range(GQ):
                        act.wait_ge(h_ps, GQ * k + 1 + q)
                        since(act, gl_r, GQ * (k - 1) + 1 + q)
                        act.activation(g_s[q], ps_h[:, q, :], ACT.Gelu, scale=1.0 / (X_SCALE * W_SCALE)).then_inc(g_r, 1)
                k, half, b = here(j, u, 0)
                if moe_valid(k):
                    act.wait_ge(y_ps, k + 1)
                    since(act, scat[b], 16 * SUBS * half)
                    act.activation(y_s[b], ps_y[:, b, :], ACT.Copy, scale=1.0 / (G_SCALE * W_SCALE)).then_inc(y_r, 1)
            moe(-1, 1)
            moe_steps(act, 0, moe)

            def group(j, u):
                g, half, b = here(j, u, 0)
                if group_valid(g):
                    since(act, c_out, g - 1)
                    act.wait_ge(yin[b], 16 * TOPK * (half + 1))
                    for r in range(CG):
                        act.activation(f_s[b][:, r, :], y_in[b][:, 0, r, :], ACT.Copy, scale=mix_w[:, 0, bass.ds(CG * g + r, 1)]).then_inc(c_f0, 1)
            group_steps(act, 0, GROUPS, group)

        @block.gpsimd
        def _(pool):
            pool.memset(neg_half[:, :], -0.5).then_inc(power_r, 1)
            pool.memset(eps[:, :], LN_EPS).then_inc(power_r, 1)
            pool.wait_ge(power_r, 2)
            pool.wait_ge(loaded, ALL_LOADED)

            def rstd(t, mv, ve, ve_r, rs, rs_r):
                pool.tensor_tensor(ve, mv[:, 1:2], eps[:, 0:1], ALU.add).then_inc(ve_r, 1)
                pool.wait_ge(ve_r, t + 1)
                pool.tensor_tensor(rs, ve, neg_half[:, 0:1], ALU.pow).then_inc(rs_r, 1)

            def step(j, u):
                t, half, b = here(j, u, -3)
                if valid(t):
                    pool.wait_ge(mv2_r, t + 1)
                    since(pool, rs2_r, t)
                    since(pool, xn2_r, t - 1)
                    rstd(t, mv2[b], ve2, ve2_r, rs2[b], rs2_r)
                t, half, b = here(j, u, 3)
                if valid(t):
                    pool.wait_ge(mv1_r, t + 1)
                    since(pool, xn_r, t - 1)
                    since(pool, rs1_r, t)
                    rstd(t, mv1[b], ve1, ve1_r, rs1[b], rs1_r)
                t, half, b = here(j, u, 1)
                if valid(t):
                    pool.wait_ge(xn_r, t + 1)
                    r = resid[:, bass.ds(t, 1), :].rearrange("p a d -> p (a d)")
                    pool.tensor_tensor(r, r, bo_s, ALU.add).then_inc(bo_added, 1)
                t, half, b = here(j, u, 1)
                if valid(t):
                    pool.wait_ge(qb_r, t + 1)
                    since(pool, s_ps, t)
                    pool.tensor_tensor(q_m.rearrange("p c b h q -> p (c b) h q"),
                                       q_b.rearrange("p c (b q) -> p (c b) q", b=NB).unsqueeze(2).to_broadcast([P, HC * NB, 2, BLOCK]),
                                       cst[:, C_MASK:C_MASK + 2].unsqueeze(1).unsqueeze(3).to_broadcast([P, HC * NB, 2, BLOCK]),
                                       ALU.mult).then_inc(q_r, 1)
                t, half, b = here(j, u, -1)
                if valid(t):
                    cols = bass.ds(t * WCOLS, WCOLS)
                    pool.wait_ge(w_hi_r, t + 1)
                    pool.tensor_tensor(w_lo[:, cols], staging[b], w_hi[:, cols], ALU.subtract).then_inc(w_lo_r, 1)
                t, half, b = here(j, u, -3)
                if valid(t):
                    pool.wait_ge(xn2_r, t + 1)
                    r = resid[:, bass.ds(t, 1), :].rearrange("p a d -> p (a d)")
                    pool.tensor_tensor(r, r, xn2, ALU.add).then_inc(xn2_added, 1)
            for i in range(-3, 0):
                step(i // 2, i % 2)
            steps(pool, 0, step)

            for c in range(TOPK * TILES // RG):
                pool.wait_ge(rt_unit, c + 1)
                if c >= 2:
                    pool.wait_ge(rt_grp_used, c - 1)
                pool.tensor_tensor(tile_val[c % 2], is_tile[c % 2],
                                   rc[:, R_VAL + c * RG:R_VAL + (c + 1) * RG].unsqueeze(2).to_broadcast([P, RG, UNITS]),
                                   ALU.mult).then_inc(rt_grp, 1)

            pool.wait_ge(routed, 1)
            for b in range(2):
                pool.wait_ge(xn2_out[b], 16 * TILES // 2)

            def moe(j, u):
                k, half, b = here(j, u, 3)
                if moe_valid(k):
                    since(pool, gt_ps, k - 1)
                    since(pool, gat[b], 16 * SUBS * half)
                    pool.tensor_copy(gidx[b], slot_token[:, bass.ds(SUBS * k, SUBS)]).then_inc(gidx_r, 1)
                    pool.wait_ge(gidx_r, k + 1)
                    settled(pool)
                    for v in range(SUBS):
                        pool.indirect_dma_start(xg[b][:, v, :], None, xn_rows[:, :],
                                                bass.IndirectOffsetOnAxis(ap=gidx[b][:, v:v + 1], axis=0)).then_inc(gat[b], 16)
                k, half, b = here(j, u, -1)
                if moe_valid(k):
                    since(pool, scat[b], 16 * SUBS * half)
                    pool.tensor_copy(didx[b], slot_dest[:, bass.ds(SUBS * k, SUBS)]).then_inc(didx_r, 1)
                    pool.wait_ge(didx_r, k + 1)
                    pool.wait_ge(y_r, k + 1)
                    settled(pool)
                    for v in range(SUBS):
                        pool.indirect_dma_start(y_rows[:, :], bass.IndirectOffsetOnAxis(ap=didx[b][:, v:v + 1], axis=0),
                                                y_s[b][:, v * D:(v + 1) * D], None).then_inc(scat[b], 16)
            for k in range(-3, 0):
                moe(k // 2, k % 2)
            moe_steps(pool, 0, moe)

            def group(j, u):
                g, half, b = here(j, u, 0)
                if group_valid(g):
                    since(pool, c_rsr, g)
                    since(pool, c_ap, CG * (g - 1))
                    pool.wait_ge(c_mvr, CG * (g + 1))
                    pool.tensor_tensor(c_ve.unsqueeze(2), c_mv[b][:, :, 1:2], eps[:, :].unsqueeze(2), ALU.add).then_inc(c_ver, 1)
                    pool.wait_ge(c_ver, g + 1)
                    pool.tensor_tensor(c_rs[b], c_ve, neg_half[:, :], ALU.pow).then_inc(c_rsr, 1)
                g, half, b = here(j, u, -1)
                if group_valid(g):
                    pool.wait_ge(c_ap, CG * (g + 1))
                    since(pool, outs[b], 16 * half)
                    pool.tensor_tensor(o_s[b], f_s[b], resid[:, bass.ds(CG * g, CG), :], ALU.add).then_inc(c_out, 1)
            group_steps(pool, 0, GROUPS + 1, group)


def kernel(x, ctx_1024, L0_xattn_Wq, L0_xattn_bq, L0_xattn_Wk, L0_xattn_bk, L0_xattn_Wv, L0_xattn_bv, L0_xattn_Wo, L0_xattn_bo,
           L0_ffn_gate_w, L0_ffn_expert_bias, L0_ffn_w_up, L0_ffn_w_down):
    import concourse.bacc as bacc
    from concourse.bass_utils import run_bass_kernel_spmd

    rows = lambda w: np.asarray(w).reshape(HC, P, -1).transpose(1, 0, 2)
    heads = (HC, STRIPS, 2, DK)
    up = np.asarray(L0_ffn_w_up).transpose(0, 2, 1).reshape(E, HC, P, I)
    down = np.asarray(L0_ffn_w_down).transpose(0, 2, 1).reshape(E, 2, IC // 2, P, D).transpose(0, 1, 3, 2, 4).reshape(E, 2, P, WCOLS)
    consts, route_consts = constants()
    arrays = {
        "x_in": np.asarray(x).reshape(TILES, P, D),
        "ctx_t": np.asarray(ctx_1024).reshape(TILES, P, HC, P).transpose(0, 3, 2, 1),
        "wq": rows(L0_xattn_Wq), "wk": rows(L0_xattn_Wk), "wv": rows(L0_xattn_Wv),
        "wo": np.asarray(L0_xattn_Wo).reshape(*heads, D).transpose(1, 0, 3, 2, 4).reshape(P, 2, D),
        "bq": np.asarray(L0_xattn_bq).reshape(HC, P).T, "bk": np.asarray(L0_xattn_bk).reshape(HC, P).T,
        "bv": np.asarray(L0_xattn_bv).reshape(heads).transpose(1, 0, 3, 2).reshape(P, 2),
        "bo": np.broadcast_to(np.asarray(L0_xattn_bo), (P, D)),
        "gate_t": rows(np.asarray(L0_ffn_gate_w).T), "gate_b": np.broadcast_to(np.asarray(L0_ffn_expert_bias), (P, E)),
        "weights": np.concatenate([up, down], 1).reshape(WSTEPS, P, WCOLS),
        "consts": consts, "route_consts": route_consts,
    }
    arrays = {n: np.ascontiguousarray(a) for n, a in arrays.items()}
    nc = bacc.Bacc("TRN2", target_bir_lowering=False, num_devices=1)
    args = [nc.dram_tensor(n, a.shape, mybir.dt.from_np(a.dtype), kind="ExternalInput").ap() for n, a in arrays.items()]
    out = nc.dram_tensor("out", (TILES, P, D), F32, kind="ExternalOutput").ap()
    program(nc, *args, out)
    r = run_bass_kernel_spmd(nc, [arrays], core_ids=[0])
    return r.results[0]["out"].reshape(BATCH, SEQ, D)
```

```python
from contextlib import ExitStack

import numpy as np

import concourse.bass as bass
from concourse import mybir

F32 = mybir.dt.float32
F16 = mybir.dt.float16
I32 = mybir.dt.int32
ALU = mybir.AluOpType
ACT = mybir.ActivationFunctionType
AX = mybir.AxisListType

P = 128
BATCH, SEQ, D = 8, 512, 256
TOKENS = BATCH * SEQ
TILES = TOKENS // P
HC = D // P
HEADS, DK, BLOCK = 16, 16, 64
PAIRS = HEADS // 2
STRIPS = 4
NB = P // BLOCK
E, I, TOPK = 8, 1024, 2
IC = I // P
SUBS = 2
SLOTS = SUBS * P
SLOT_TILES = TOKENS * TOPK // SLOTS + E - 1
UNITS = SUBS * SLOT_TILES
WSTEPS = 4 * E
WCOLS = HC * I // 2
EXPERT_COLS = HC * I
X_SCALE = 2048.0
W_SCALE = 256.0
G_SCALE = 256.0
CTX_SCALE = 64.0
LN_EPS = 1e-5
GATE_EPS = 1e-6
VCOLS = 2 * DK + 1

C_ID, C_MASK, C_BQ, C_BK, C_BV, C_GATE, C_GATE_B, C_END = np.cumsum([0, P, 2, HC, HC, 2, HC * E, E]).tolist()
R_TRI, R_ONES, R_IOTA, R_DESC, R_GRP, R_P, R_STEP, R_PAD, R_END = np.cumsum(
    [0, P, P, P, E * TILES, TOPK * TILES, 1, TILES, UNITS]).tolist()


def constants():
    c, r = np.zeros((P, C_BQ), np.float32), np.zeros((P, R_END), np.float32)
    p = np.arange(P)
    c[:, C_ID:C_ID + P] = np.eye(P)
    c[:, C_MASK:C_MASK + 2] = (p[:, None] // DK % 2) == np.arange(2)[None]
    r[:, R_TRI:R_TRI + P] = p[:, None] < p[None, :]
    r[:, R_ONES:R_ONES + P] = 1
    r[:, R_IOTA:R_IOTA + P] = p[None, :]
    r[:, R_DESC:R_DESC + E * TILES] = (E - np.arange(E * TILES) // TILES)[None]
    g = np.arange(TOPK * TILES)
    r[:, R_GRP:R_GRP + g.size] = g[None] - TOPK * TILES
    r[:, R_P] = p
    r[:, R_STEP:R_STEP + TILES] = (SLOTS * np.arange(TILES))[None]
    r[:, R_PAD:R_PAD + UNITS] = p[:, None] + P * (np.arange(UNITS) % (2 * SUBS))[None]
    return c, r


def program(nc, x, ctx_t, w_qk, w_vo, bo, weights, small, route_consts, out):
    es = ExitStack()
    with es:
        def sb(name, shape, dt=F32):
            return es.enter_context(nc.sbuf_tensor(name, shape, dt))

        def sem(name):
            return es.enter_context(nc.semaphore(name))

        xn_rows = nc.dram_tensor("xn_rows", [TOKENS, D], F32, kind="Internal").ap()
        y_rows = nc.dram_tensor("y_rows", [TOPK * TOKENS + 2 * SLOTS, D], F32, kind="Internal").ap()

        resid = sb("resid", [P, TILES, D])
        w_hi = sb("w_hi", [P, 2 * E * EXPERT_COLS], F16)
        w_lo = sb("w_lo", [P, 2 * E * EXPERT_COLS], F16)
        cst = sb("cst", [P, C_END])
        logits = sb("logits", [P, E, TILES])
        mix_w = sb("mix_w", [P, TOPK, TILES])
        slot_dest = sb("slot_dest", [P, UNITS], I32)
        slot_token = sb("slot_token", [P, UNITS], I32)
        slot_expert = sb("slot_expert", [P, SLOT_TILES], I32)

        ident = cst[:, C_ID:C_ID + P]
        bq_s, bk_s, bv_s = (cst[:, n:n + 2] for n in (C_BQ, C_BK, C_BV))
        gate_w = cst[:, C_GATE:C_GATE_B].rearrange("p (c e) -> p c e", c=HC)
        gate_bias = cst[:, C_GATE_B:C_END]

        AREA = 11500
        area = sb("area", [P, AREA])
        at = [0]

        def carve(cols, dt=F32):
            n = cols if dt != F16 else cols // 2
            v = area[:, at[0]:at[0] + n]
            at[0] += n
            assert at[0] <= AREA, at[0]
            return v if dt == F32 else v.bitcast(dt)

        w_qk_s, wo_flat = carve(2 * HC * D), carve(HC * D)
        wq_s, wk_s, wo_s = (w.rearrange("p (c n) -> p c n", c=HC) for w in (w_qk_s[:, 0:HC * D], w_qk_s[:, HC * D:2 * HC * D], wo_flat))
        bo_s = carve(D)
        staging_at = at[0]
        staging = [carve(WCOLS) for _ in range(2)]
        xn = carve(D)
        xn_t = xn2_t = carve(D).rearrange("p (c n) -> p c n", c=HC)
        wv_hi, wv_lo = (carve(HC * D, F16).rearrange("p (c n) -> p c n", c=HC) for _ in range(2))
        ctx_hi, ctx_lo = (carve(D, F16).rearrange("p (c n) -> p c n", c=HC) for _ in range(2))
        ctx = [carve(D).rearrange("p (c n) -> p c n", c=HC) for _ in range(2)]
        q_m = carve(HC * 2 * P).rearrange("p (c b h n) -> p c b h n", c=HC, b=NB, h=2)
        q_b = carve(HC * P).rearrange("p (c n) -> p c n", c=HC)
        k_bd = carve(HC * NB * STRIPS * BLOCK).rearrange("p (c b s k) -> p c b s k", c=HC, b=NB, s=STRIPS)
        v_x = [carve(PAIRS * NB * VCOLS).rearrange("p (s c b x) -> p s c b x", s=STRIPS, c=HC, b=NB) for _ in range(2)]
        prob = carve(PAIRS * P)
        prob_t_flat = carve(PAIRS * P)
        prob_t = prob_t_flat.rearrange("p (h n) -> p h n", h=PAIRS)
        wv_flat = prob_t_flat[:, 0:HC * D]
        wv_s = wv_flat.rearrange("p (c n) -> p c n", c=HC)
        o_n = carve(D).rearrange("p (b n) -> p b n", b=NB)
        o_t = carve(D).rearrange("p (h n) -> p h n", h=2)
        xn2 = carve(D)
        row_max = carve(PAIRS * NB)
        o_sum = carve(PAIRS * NB)
        stats1, stats2 = carve(6), carve(6)
        mv1, mv2 = [carve(2) for _ in range(2)], [carve(2) for _ in range(2)]
        ve1, ve2 = carve(1), carve(1)
        rs1, rs2 = [carve(1) for _ in range(2)], [carve(1) for _ in range(2)]

        at[0] = staging_at
        rc = carve(R_END)
        at[0] = staging_at + WCOLS
        RG = 8
        count_rep = carve(RG * P, F16).rearrange("p (s g) -> p s g", g=RG)
        keep = carve(E * TILES).rearrange("p (e t) -> p e t", e=E)
        at[0] = staging_at + 2 * WCOLS

        def etv():
            return carve(E * TILES).rearrange("p (e t) -> p e t", e=E)
        lg_s, ex, eq, oh1, oh2, pos, base, incl, mk = (etv() for _ in range(9))
        lmax, lsum, lrec, m1, m2, i1, i2, den, drec = (carve(TILES) for _ in range(9))
        tiles_e, tin, tex = carve(E), carve(E), carve(E)
        pos_j = carve(TOPK * TILES)
        pos_i, tile_i, slot_i = (carve(TOPK * TILES).bitcast(I32) for _ in range(3))
        tile_f, slot_f = carve(TOPK * TILES, F16), carve(TOPK * TILES, F16)
        is_slot = [carve(RG * P, F16).rearrange("p (s g) -> p s g", g=RG) for _ in range(2)]
        is_tile = [carve(RG * UNITS, F16).rearrange("p (s g) -> p s g", g=RG) for _ in range(2)]
        tile_val = [carve(RG * 2 * UNITS, F16).rearrange("p (v s g) -> p v s g", g=RG, v=2) for _ in range(2)]
        ecmp = carve(SLOT_TILES * (E - 1)).rearrange("p (k e) -> p k e", e=E - 1)
        ecount = carve(SLOT_TILES)
        pair_f, pad_p, dest_f = (carve(UNITS) for _ in range(3))

        at[0] = 0
        xg = [carve(SUBS * D).rearrange("p (u n) -> p u n", u=SUBS) for _ in range(2)]
        xt_hi, xt_lo = ([carve(HC * SLOTS, F16).rearrange("p (c n) -> p c n", c=HC) for _ in range(2)] for _ in range(2))
        GQ = 4
        g_s = [carve(512) for _ in range(GQ)]
        g_hi, g_lo = ([carve(IC * SLOTS, F16).rearrange("p (c n) -> p c n", c=IC) for _ in range(2)] for _ in range(2))
        y_s = [carve(SUBS * D) for _ in range(2)]
        gidx, didx = ([carve(SUBS).bitcast(I32) for _ in range(2)] for _ in range(2))

        CG = 2
        GROUPS = TILES // CG
        y_in = w_hi[:, :].bitcast(F32).rearrange("p (g j n) -> p g j n", g=GROUPS, j=TOPK)
        f_s, o_s = (w_lo[:, h * 2 * TILES * D:(h + 1) * 2 * TILES * D].bitcast(F32).rearrange("p (t n) -> p t n", t=TILES) for h in range(2))
        at[0] = 0
        c_st = [carve(CG * 6).rearrange("p (t n) -> p t n", t=CG) for _ in range(4)]
        c_mv = [carve(CG * 2).rearrange("p (t n) -> p t n", t=CG) for _ in range(4)]
        c_ve, c_rs, c_nm = (carve(TILES) for _ in range(3))
        neg_half, eps, warm = sb("neg_half", [P, CG]), sb("eps", [P, CG]), sb("warm", [P, 1])

        ps_a = es.enter_context(nc.psum_tensor("ps_a", [P, 4, 512], F32))
        ps_b = es.enter_context(nc.psum_tensor("ps_b", [P, 2, 512], F32))
        ps_c = es.enter_context(nc.psum_tensor("ps_c", [P, 2, 512], F32))
        ps_s = ps_a[:, 0:2, :].rearrange("p a (x s k) -> p (a x) s k", s=STRIPS, k=BLOCK)
        half_bank = lambda m, h: ps_c[:, m, h * 256:(h + 1) * 256].rearrange("p (c n) -> p c n", c=HC)
        ps_v = ps_a[:, 2, 0:D]
        ps_x2t = ps_a[:, 2, D:2 * D].rearrange("p (c n) -> p c n", c=HC)
        ps_wo, ps_lg = ps_a[:, 3, 0:D], ps_a[:, 3, D:D + E]
        ps_xt = ps_ot = half_bank(0, 0)
        ps_q, ps_k = half_bank(1, 0), half_bank(1, 1)
        ps_pt = ps_b[:, :, :].rearrange("p a (h n) -> p (a h) n", n=P)
        ps_o = ps_b[:, :, 0:4 * NB * VCOLS].rearrange("p a (y x) -> p a y x", x=VCOLS)
        ps_wo_last = ps_a[:, 0, 0:D]
        ps_h = ps_a
        ps_y = ps_b
        ps_x = ps_c

        small_in, qk_in, rest_in = sem("small_in"), sem("qk_in"), sem("rest_in")
        x_in = [sem(f"x_in{i}") for i in range(2)]
        ctx_in = [sem(f"ctx_in{i}") for i in range(2)]
        w_in = [sem(f"w_in{i}") for i in range(2)]
        xn2_out = [sem(f"xn2_out{i}") for i in range(2)]
        zeroed = sem("zeroed")
        st1, mv1_r, ve1_r, rs1_r, xn_r = (sem(n) for n in ("st1", "mv1_r", "ve1_r", "rs1_r", "xn_r"))
        st2, mv2_r, ve2_r, rs2_r, xn2_r = (sem(n) for n in ("st2", "mv2_r", "ve2_r", "rs2_r", "xn2_r"))
        bo_added, x1_r, xn2_added = sem("bo_added"), sem("x1_r"), sem("xn2_added")
        xt_ps, xt_r = sem("xt_ps"), sem("xt_r")
        wv_scaled, wv_hi_r, wv_lo_r, ctx_scaled, ctx_hi_r, ctx_lo_r = (
            sem(n) for n in ("wv_scaled", "wv_hi_r", "wv_lo_r", "ctx_scaled", "ctx_hi_r", "ctx_lo_r"))
        q_r, qb_r, k_ps, k_r, v_ps, v_r = (sem(n) for n in ("q_r", "qb_r", "k_ps", "k_r", "v_ps", "v_r"))
        s_ps, max_r, sub_r, p_r, pt_ps, pt_r = (sem(n) for n in ("s_ps", "max_r", "sub_r", "p_r", "pt_ps", "pt_r"))
        o_ps, osum_r, o_r, ot_ps, ot_r, wo_ps = (sem(n) for n in ("o_ps", "osum_r", "o_r", "ot_ps", "ot_r", "wo_ps"))
        x2t_ps, x2t_r, lg_ps, lg_r = (sem(n) for n in ("x2t_ps", "x2t_r", "lg_ps", "lg_r"))
        w_scaled, w_hi_r, w_lo_r = sem("w_scaled"), sem("w_hi_r"), sem("w_lo_r")

        def here(j, u, skew):
            return 2 * j + (u + skew), j + (u + skew) // 2, (u + skew) % 2

        def valid(t):
            return not isinstance(t, int) or 0 <= t < TILES

        FIRST, LAST = 6, TILES - 6

        def steps(eng, lo, step):
            for i in range(lo, FIRST):
                step(i // 2, i % 2)
            with eng.Fori(0, (LAST - FIRST) // 4) as n:
                for u in range(4):
                    step(2 * n + FIRST // 2, u)
            for i in range(LAST, TILES + 5):
                step(i // 2, i % 2)

        def last_out(t):
            return isinstance(t, int) and t == TILES - 1

        def since(eng, s, count):
            if not isinstance(count, int) or count > 0:
                eng.wait_ge(s, count)

        passed = {n: sem(f"passed_{n}") for n in ("dve", "pool")}

        def settled(eng):
            eng.sem_inc(passed["dve" if eng.engine == nc.vector.engine else "pool"], 1)

        block = es.enter_context(nc.Block())

        rt = sem("rt")
        rt_shifted, rt_exp, rt_mask = sem("rt_shifted"), sem("rt_exp"), sem("rt_mask")
        rt_cnt = sem("rt_cnt")
        rt_slot = sem("rt_slot")
        rt_grp = sem("rt_grp")
        rt_grp_used = sem("rt_grp_used")
        rt_made = sem("rt_made")
        rt_pos = sem("rt_pos")
        rt_unit = sem("rt_unit")
        routed = sem("routed")
        gat = [sem(f"gat{i}") for i in range(2)]
        scat = [sem(f"scat{i}") for i in range(2)]
        gidx_r, didx_r = sem("gidx_r"), sem("didx_r")
        gt_ps, xh_r, xl_r, h_ps, g_r, gh_r, gl_r, y_ps, y_r = (
            sem(n) for n in ("gt_ps", "xh_r", "xl_r", "h_ps", "g_r", "gh_r", "gl_r", "y_ps", "y_r"))
        rc_in = sem("rc_in")
        power_r = sem("power_r")
        yin = [sem(f"yin{i}") for i in range(4)]
        outs = sem("outs")
        c_f0, c_f1, c_stats, c_mvr, c_ver, c_rsr, c_nmr, c_ap, c_out = (
            sem(n) for n in ("c_f0", "c_f1", "c_stats", "c_mvr", "c_ver", "c_rsr", "c_nmr", "c_ap", "c_out"))

        MOE_FIRST, MOE_LAST = 4, 36

        def moe_steps(eng, lo, step):
            for k in range(lo, MOE_FIRST):
                step(k // 2, k % 2)
            with eng.Fori(MOE_FIRST // 2, MOE_LAST // 2) as j:
                step(j, 0)
                step(j, 1)
            for k in range(MOE_LAST, SLOT_TILES + 1):
                step(k // 2, k % 2)

        def moe_valid(k):
            return not isinstance(k, int) or 0 <= k < SLOT_TILES

        def group_steps(eng, step, last=GROUPS):
            for g in range(4):
                step(g, 0, g)
            with eng.Fori(1, last // 4) as j:
                for u in range(4):
                    step(4 * j + u, j, u)
            for g in range(last, GROUPS + 4):
                step(g, g // 4, g % 4)

        def group_valid(g):
            return not isinstance(g, int) or 0 <= g < GROUPS

        @block.sync
        def _(sp):
            def step(j, u):
                t, half, b = here(j, u, 3)
                if valid(t):
                    since(sp, x_in[b], 16 * half)
                    sp.dma_start(resid[:, bass.ds(t, 1), :], x[bass.ds(t, 1)].rearrange("a p d -> p a d")).then_inc(x_in[b], 16)
                t, half, b = here(j, u, 1)
                if valid(t):
                    since(sp, v_ps, t - 1)
                    sp.dma_start(ctx[b], ctx_t[bass.ds(t, 1)].rearrange("a p c n -> p (a c) n")).then_inc(ctx_in[b], 16)
                t, half, b = here(j, u, 1)
                if valid(t):
                    since(sp, w_lo_r, t - 1)
                    sp.dma_start(staging[b], weights[bass.ds(t, 1)].rearrange("a p n -> p (a n)")).then_inc(w_in[b], 16)
                t, half, b = here(j, u, -3)
                if valid(t):
                    sp.wait_ge(xn2_r, t + 1)
                    sp.dma_start(xn_rows[bass.ds(t * P, P), :], xn2).then_inc(xn2_out[b], 16)
                if isinstance(j, int) and 2 * j + u == TILES:
                    sp.wait_ge(w_lo_r, WSTEPS)
                    sp.dma_start(rc, route_consts).then_inc(rc_in, 16)
            for i in range(-3, 0):
                step(i // 2, i % 2)
            steps(sp, 0, step)

            sp.wait_ge(scat[0], 16 * SUBS * ((SLOT_TILES + 1) // 2))
            sp.wait_ge(scat[1], 16 * SUBS * (SLOT_TILES // 2))
            sp.wait_ge(y_ps, SLOT_TILES)
            y_two = y_rows[0:TOPK * TOKENS, :].rearrange("(j g t p) d -> g j p t d", j=TOPK, t=CG, p=P)
            out_g = out.rearrange("(g t) p d -> g p t d", t=CG)

            def load(g, u):
                for c in range(TOPK):
                    sp.dma_start(y_in[:, bass.ds(g, 1), c].rearrange("p a (t d) -> p (a t) d", t=CG),
                                 y_two[bass.ds(g, 1), c].rearrange("a p t d -> p (a t) d")).then_inc(yin[u], 16)
            for g in range(4):
                load(g, g)

            def group(g, j, u):
                if not isinstance(g, int) or g < GROUPS - 4:
                    sp.wait_ge(yin[u], 16 * TOPK * (j + 1))
                    load(g + 4, u)
                g = g - 4
                if group_valid(g):
                    sp.wait_ge(c_out, g + 1)
                    sp.dma_start(out_g[bass.ds(g, 1)].rearrange("a p t d -> p (a t) d"), o_s[:, bass.ds(CG * g, CG), :]).then_inc(outs, 16)
            group_steps(sp, group, GROUPS - 4)
            sp.wait_ge(outs, 16 * GROUPS)

        @block.tensor
        def _(pe):
            pe.wait_ge(small_in, 16)
            pe.wait_ge(zeroed, 4)

            def step(j, u):
                t, half, b = here(j, u, 1)
                if valid(t):
                    pe.wait_ge(xn_r, t + 1)
                    since(pe, ot_r, 2 * (t - 3))
                    for c in range(HC):
                        mm = pe.transpose(ps_xt[:, c, :], xn[:, c * P:(c + 1) * P], ident)
                    mm.then_inc(xt_ps, 1)
                t, half, b = here(j, u, 0)
                if valid(t):
                    pe.wait_ge(q_r, t + 1)
                    pe.wait_ge(k_r, STRIPS * (t + 1))
                    since(pe, sub_r, t)
                    for c in range(HC):
                        for n in range(NB):
                            mm = pe.matmul(ps_s[:, c * NB + n, :, :].rearrange("p s k -> p (s k)"),
                                           q_m[:, c, n].rearrange("p h q -> p (h q)"),
                                           k_bd[:, c, n].rearrange("p s k -> p (s k)"), start=True, stop=True)
                    mm.then_inc(s_ps, 1)
                t, half, b = here(j, u, -1)
                if valid(t):
                    pe.wait_ge(p_r, t + 1)
                    since(pe, o_r, 4 * t)
                    for h in range(PAIRS):
                        mm = pe.transpose(ps_pt[:, h, :], prob[:, h * P:(h + 1) * P], ident)
                    mm.then_inc(pt_ps, 1)
                t, half, b = here(j, u, 1)
                if valid(t):
                    if isinstance(t, int) and t == 0:
                        pe.wait_ge(qk_in, 16)
                    pe.wait_ge(xt_r, t + 1)
                    since(pe, qb_r, t)
                    since(pe, k_r, STRIPS * t)
                    for c in range(HC):
                        for k in range(HC):
                            mm = pe.matmul(ps_q[:, c, :], wq_s[:, k, c * P:(c + 1) * P], xn_t[:, k, :],
                                           start=(k == 0), stop=(k == HC - 1))
                    pe.wait_ge(ctx_in[b], 16 * (half + 1))
                    for c in range(HC):
                        for k in range(HC):
                            mm = pe.matmul(ps_k[:, c, :], wk_s[:, k, c * P:(c + 1) * P], ctx[b][:, k, :],
                                           start=(k == 0), stop=(k == HC - 1))
                    mm.then_inc(k_ps, 1)
                t, half, b = here(j, u, -2)
                if valid(t):
                    pe.wait_ge(o_r, 4 * (t + 1))
                    for n in range(NB):
                        mm = pe.transpose(ps_ot[:, n, :], o_n[:, n, :], ident)
                    mm.then_inc(ot_ps, 1)
                t, half, b = here(j, u, -1)
                if valid(t):
                    pe.wait_ge(pt_r, t + 1)
                    pe.wait_ge(v_r, 2 * (t + 1))
                    for h in range(PAIRS):
                        mm = pe.matmul(ps_o[:, h // 4, (h % 4) * NB:(h % 4 + 1) * NB, :], prob_t[:, h, :],
                                       v_x[b][:, h // HC, h % HC, :, :], start=True, stop=True)
                    mm.then_inc(o_ps, 1)
                def rows_for_gate():
                    t, half, b = here(j, u, -3)
                    if valid(t):
                        pe.wait_ge(xn2_r, t + 1)
                        since(pe, x2t_r, t)
                        since(pe, v_r, 2 * (min(t + 3, TILES) if isinstance(t, int) else t + 3))
                        for c in range(HC):
                            mm = pe.transpose(ps_x2t[:, c, :], xn2[:, c * P:(c + 1) * P], ident)
                        mm.then_inc(x2t_ps, 1)
                if not last_out(here(j, u, -2)[0]):
                    rows_for_gate()
                t, half, b = here(j, u, 0)
                if valid(t):
                    pe.wait_ge(ctx_lo_r, t + 1)
                    since(pe, v_r, 2 * t)
                    n = 0
                    for k in range(HC):
                        for c, w in ((ctx_hi, wv_hi), (ctx_hi, wv_lo), (ctx_lo, wv_hi)):
                            mm = pe.matmul(ps_v, c[:, k, :], w[:, k, :], start=(n == 0), stop=(n == 3 * HC - 1))
                            n += 1
                    mm.then_inc(v_ps, 1)
                t, half, b = here(j, u, -2)
                if valid(t):
                    pe.wait_ge(ot_r, 2 * (t + 1))
                    if last_out(t):
                        pe.wait_ge(sub_r, TILES)
                    else:
                        since(pe, x1_r, t)
                        since(pe, lg_r, t - 1)
                    for h in range(2):
                        mm = pe.matmul(ps_wo_last if last_out(t) else ps_wo, o_t[:, h, :], wo_s[:, h, :], start=(h == 0), stop=(h == 1))
                    mm.then_inc(wo_ps, 1)
                if last_out(t):
                    rows_for_gate()
                t, half, b = here(j, u, -3)
                if valid(t):
                    pe.wait_ge(x2t_r, t + 1)
                    pe.wait_ge(x1_r, t + 1)
                    since(pe, lg_r, t)
                    for k in range(HC):
                        mm = pe.matmul(ps_lg, xn2_t[:, k, :], gate_w[:, k, :], start=(k == 0), stop=(k == HC - 1))
                    mm.then_inc(lg_ps, 1)
            step(-1, 1)
            pe.wait_ge(rest_in, 48)
            pe.wait_ge(wv_lo_r, 1)
            steps(pe, 0, step)

            pe.wait_ge(rt_mask, 1)
            pe.wait_ge(rc_in, 16)
            pe.matmul(ps_b[:, 0, 0:E * TILES], rc[:, R_TRI:R_TRI + P], mk.rearrange("p e t -> p (e t)"), start=True, stop=True)
            pe.matmul(ps_b[:, 1, 0:E * TILES], rc[:, R_ONES:R_ONES + P], mk.rearrange("p e t -> p (e t)"),
                      start=True, stop=True).then_inc(rt_cnt, 1)
            for g in range(TOPK * TILES):
                if g % RG == 0:
                    pe.wait_ge(rt_grp, g // RG + 1)
                    pe.wait_ge(rt_pos, g // RG + 1)
                    pe.wait_ge(rt_slot, g // RG + 1)
                mm = pe.matmul(ps_c[:, 0, 0:2 * UNITS], is_slot[g // RG % 2][:, :, g % RG],
                               tile_val[g // RG % 2].rearrange("p v s g -> p (v s) g")[:, :, g % RG],
                               start=(g == 0), stop=(g == TOPK * TILES - 1))
                if g % RG == RG - 1:
                    mm.then_inc(rt_grp_used, 1)

            pe.wait_ge(routed, 1)
            pe.wait_ge(w_lo_r, WSTEPS)

            def transpose_rows(k, half, b):
                pe.wait_ge(gat[b], 16 * SUBS * (half + 1))
                since(pe, xl_r, k - 1)
                for c in range(HC):
                    for v in range(SUBS):
                        at = c * SLOTS + v * P
                        mm = pe.transpose(ps_x[:, b, at:at + P], xg[b][:, v, c * P:(c + 1) * P], ident)
                mm.then_inc(gt_ps, 1)

            def expert_of(k):
                e = pe.value_load(slot_expert[0:1, bass.ds(k, 1)], min_val=0, max_val=E - 1)
                return pe.snap(e * (2 * EXPERT_COLS))

            def up(k, b, first, quarters=range(GQ)):
                pe.wait_ge(xl_r, k + 1)
                for ic in range(quarters[0] * IC // GQ, (quarters[-1] + 1) * IC // GQ):
                    q = ic // 2
                    if ic % 2 == 0:
                        since(pe, g_r, GQ * (k - 1) + q + 1)
                    n = 0
                    for hc in range(HC):
                        for w, r in ((w_hi, xt_hi), (w_hi, xt_lo), (w_lo, xt_hi)):
                            mm = pe.matmul(ps_h[:, q, (ic % 2) * SLOTS:(ic % 2 + 1) * SLOTS],
                                           w[:, bass.ds(first + (hc * I + ic * P), P)], r[b][:, hc, :],
                                           start=(n == 0), stop=(n == 3 * HC - 1))
                            n += 1
                    if ic % 2:
                        mm.then_inc(h_ps, 1)

            def down(k, b, first):
                since(pe, y_r, k - 1)
                pe.wait_ge(gl_r, GQ * (k + 1))
                for v in range(SUBS):
                    n = 0
                    for ic in range(IC):
                        for g, w in ((g_hi, w_hi), (g_lo, w_hi), (g_hi, w_lo)):
                            mm = pe.matmul(ps_y[:, b, v * D:(v + 1) * D], g[b][:, ic, v * P:(v + 1) * P],
                                           w[:, bass.ds(first + (EXPERT_COLS + ic * D), D)],
                                           start=(n == 0), stop=(n == 3 * IC - 1))
                            n += 1
                mm.then_inc(y_ps, 1)

            def moe(j, u):
                k, half, b = here(j, u, 2)
                if moe_valid(k):
                    transpose_rows(k, half, b)
                k, half, b = here(j, u, 1)
                if moe_valid(k):
                    up(k, b, expert_of(k))
                k, half, b = here(j, u, 0)
                if moe_valid(k):
                    down(k, b, expert_of(k))
            transpose_rows(0, 0, 0)
            first = expert_of(0)
            up(0, 0, first, range(1))
            transpose_rows(1, 0, 1)
            up(0, 0, first, range(1, GQ))
            moe_steps(pe, 0, moe)

        @block.vector
        def _(dve):
            dve.memset(v_x[0], 0.0).then_inc(zeroed, 1)
            dve.memset(v_x[1], 0.0).then_inc(zeroed, 1)
            dve.memset(k_bd.rearrange("p c b s k -> p (c b s k)"), 0.0).then_inc(zeroed, 1)
            dve.wait_ge(zeroed, 3)
            for b in range(2):
                for n in range(NB):
                    r = slice(n * BLOCK, (n + 1) * BLOCK)
                    ins = dve.memset(v_x[b][r, :, :, n, 2 * DK:VCOLS].rearrange("p s c x -> p (s c) x"), 1.0)
            ins.then_inc(zeroed, 1)

            def step(j, u):
                t, half, b = here(j, u, -3)
                if valid(t):
                    dve.wait_ge(wo_ps, t + 1)
                    if not last_out(t):
                        since(dve, lg_ps, t)
                    dve.wait_ge(bo_added, t + 1)
                    r = resid[:, bass.ds(t, 1), :].rearrange("p a d -> p (a d)")
                    dve.tensor_tensor(r, ps_wo_last if last_out(t) else ps_wo, r, ALU.add).then_inc(x1_r, 1)
                t, half, b = here(j, u, 3)
                if valid(t):
                    since(dve, mv1_r, t)
                    dve.wait_ge(x_in[b], 16 * (half + 1))
                    settled(dve)
                    dve.bn_stats(stats1, resid[:, bass.ds(t, 1), :].rearrange("p a d -> p (a d)")).then_inc(st1, 1)
                t, half, b = here(j, u, -4)
                if valid(t):
                    dve.wait_ge(lg_ps, t + 1)
                    dve.tensor_tensor(logits[:, :, bass.ds(t, 1)], ps_lg.unsqueeze(2), gate_bias.unsqueeze(2), ALU.add).then_inc(lg_r, 1)
                t, half, b = here(j, u, -3)
                if valid(t):
                    since(dve, mv2_r, t)
                    dve.wait_ge(x1_r, t + 1)
                    settled(dve)
                    dve.bn_stats(stats2, resid[:, bass.ds(t, 1), :].rearrange("p a d -> p (a d)")).then_inc(st2, 1)
                t, half, b = here(j, u, 3)
                if valid(t):
                    since(dve, ve1_r, t - 1)
                    since(dve, xn_r, t - 1)
                    dve.wait_ge(st1, t + 1)
                    settled(dve)
                    dve.bn_aggr(mv1[b], stats1).then_inc(mv1_r, 1)
                t, half, b = here(j, u, -3)
                if valid(t):
                    since(dve, ve2_r, t - 1)
                    since(dve, xn2_r, t - 1)
                    dve.wait_ge(st2, t + 1)
                    settled(dve)
                    dve.bn_aggr(mv2[b], stats2).then_inc(mv2_r, 1)
                t, half, b = here(j, u, 0)
                if valid(t):
                    since(dve, sub_r, t)
                    dve.wait_ge(s_ps, t + 1)
                    dve.tensor_reduce(row_max.rearrange("p (x s) -> p x s", s=STRIPS), ps_s, AX.X, ALU.max).then_inc(max_r, 1)
                t, half, b = here(j, u, 0)
                if valid(t):
                    dve.wait_ge(max_r, t + 1)
                    since(dve, pt_ps, t)
                    dve.tensor_tensor(prob.rearrange("p (s x k) -> p x s k", s=STRIPS, k=BLOCK), ps_s,
                                      row_max.rearrange("p (x s) -> p x s", s=STRIPS).unsqueeze(3).to_broadcast([P, HC * NB, STRIPS, BLOCK]),
                                      ALU.subtract).then_inc(sub_r, 1)
                t, half, b = here(j, u, 2)
                if valid(t):
                    dve.wait_ge(rs1_r, t + 1)
                    since(dve, xt_ps, t)
                    dve.tensor_scalar(xn, resid[:, bass.ds(t, 1), :].rearrange("p a d -> p (a d)"), mv1[b][:, 0:1], rs1[b],
                                      ALU.subtract, ALU.mult).then_inc(xn_r, 1)
                t, half, b = here(j, u, -3)
                if valid(t):
                    dve.wait_ge(rs2_r, t + 1)
                    since(dve, xn2_out[1 - b], 16 * (half + b))
                    since(dve, x2t_ps, t)
                    since(dve, xn2_added, t)
                    dve.tensor_scalar(xn2, resid[:, bass.ds(t, 1), :].rearrange("p a d -> p (a d)"), mv2[b][:, 0:1], rs2[b],
                                      ALU.subtract, ALU.mult).then_inc(xn2_r, 1)
                t, half, b = here(j, u, 1)
                if valid(t):
                    dve.wait_ge(k_ps, t + 1)
                    since(dve, q_r, t)
                    dve.tensor_tensor(q_b, ps_q, bq_s.unsqueeze(2).to_broadcast([P, HC, P]), ALU.add).then_inc(qb_r, 1)
                    for s in range(STRIPS):
                        r = slice(32 * s, 32 * s + 32)
                        dve.tensor_tensor(k_bd[r, :, :, s, :], ps_k[r].rearrange("p c (b k) -> p c b k", b=NB),
                                          bk_s[r].unsqueeze(2).unsqueeze(3).to_broadcast([32, HC, NB, BLOCK]), ALU.add).then_inc(k_r, 1)
                t, half, b = here(j, u, -1)
                if valid(t):
                    dve.wait_ge(o_ps, t + 1)
                    since(dve, ot_ps, t)
                    since(dve, o_r, 4 * t)
                    dve.reciprocal(o_sum.rearrange("p (a y) -> p a y", a=2), ps_o[:, :, :, 2 * DK]).then_inc(osum_r, 1)
                    dve.wait_ge(osum_r, t + 1)
                    for h in range(2):
                        r = slice(h * BLOCK, (h + 1) * BLOCK)
                        for m in range(NB):
                            dve.tensor_tensor(o_n[r, m, :].rearrange("p (a y d) -> p a y d", a=2, d=DK),
                                              ps_o[r].rearrange("p a (y b) x -> p a y b x", b=NB)[:, :, :, m, h * DK:(h + 1) * DK],
                                              o_sum[r].rearrange("p (a y b) -> p a y b", a=2, b=NB)[:, :, :, m:m + 1].to_broadcast([BLOCK, 2, 4, DK]),
                                              ALU.mult).then_inc(o_r, 1)
                if isinstance(j, int) and 2 * j + u == TILES + 1:
                    dve.wait_ge(rc_in, 16)
                    dve.tensor_copy(count_rep, rc[:, R_IOTA:R_IOTA + P].unsqueeze(2).to_broadcast([P, P, RG])).then_inc(rt_made, 1)
                    dve.memset(keep, 1.0).then_inc(rt_made, 1)
                    dve.wait_ge(rt_made, 2)
                    dve.memset(keep[:, :, 0:1], 0.0).then_inc(rt_made, 1)
            for i in range(-3, -1):
                step(i // 2, i % 2)
            dve.wait_ge(small_in, 16)
            step(-1, 1)
            dve.wait_ge(wv_hi_r, 1)
            dve.tensor_tensor(wv_lo, wv_s, wv_hi, ALU.subtract).then_inc(wv_lo_r, 1)
            steps(dve, 0, step)

            n = [0]

            def link(ins):
                n[0] += 1
                ins.then_inc(rt, 1)
                dve.wait_ge(rt, n[0])

            def over_e(v):
                return v.rearrange("p e t -> p t e")

            def per_t(v):
                return v.unsqueeze(1).to_broadcast([P, E, TILES])

            dve.wait_ge(lg_r, TILES)
            dve.wait_ge(ot_r, 2 * TILES)
            dve.wait_ge(x2t_r, TILES)
            dve.wait_ge(xn2_added, TILES)
            dve.wait_ge(w_lo_r, WSTEPS)
            dve.wait_ge(wo_ps, TILES)
            for b in range(2):
                dve.wait_ge(xn2_out[b], 16 * TILES // 2)
            dve.wait_ge(rt_made, 3)
            desc = rc[:, R_DESC:R_DESC + E * TILES].rearrange("p (e t) -> p e t", e=E)
            link(dve.tensor_reduce(lmax, over_e(logits[:, :, :]), AX.X, ALU.max))
            dve.tensor_tensor(lg_s, logits[:, :, :], per_t(lmax), ALU.subtract).then_inc(rt_shifted, 1)
            dve.wait_ge(rt_exp, 1)
            link(dve.tensor_reduce(lsum, over_e(ex), AX.X, ALU.add))
            link(dve.reciprocal(lrec, lsum))
            link(dve.tensor_tensor(ex, ex, per_t(lrec), ALU.mult))
            for m, i, oh in ((m1, i1, oh1), (m2, i2, oh2)):
                link(dve.tensor_reduce(m, over_e(ex), AX.X, ALU.max))
                link(dve.tensor_tensor(eq, ex, per_t(m), ALU.is_equal))
                link(dve.tensor_tensor(eq, eq, desc, ALU.mult))
                link(dve.tensor_reduce(i, over_e(eq), AX.X, ALU.max))
                link(dve.tensor_tensor(oh, desc, per_t(i), ALU.is_equal))
                if m is m1:
                    link(dve.scalar_tensor_tensor(ex, oh, -4.0, ex, ALU.mult, ALU.add))
            dve.tensor_tensor(mk, oh1, oh2, ALU.add).then_inc(rt_mask, 1)
            link(dve.scalar_tensor_tensor(den, m1, GATE_EPS, m2, ALU.add, ALU.add))
            link(dve.reciprocal(drec, den))
            link(dve.tensor_tensor(mix_w[:, 0, :], m1, drec, ALU.mult))
            link(dve.tensor_tensor(mix_w[:, 1, :], m2, drec, ALU.mult))
            dve.wait_ge(rt_cnt, 1)
            flat = lambda v: v.rearrange("p e t -> p (e t)")
            totals = ps_b[:, 1, 0:E * TILES]
            link(dve.tensor_tensor_scan(flat(incl), flat(keep), totals, 0.0, ALU.mult, ALU.add))
            link(dve.tensor_tensor(flat(base), flat(incl), totals, ALU.subtract))
            first_slots = rc[:, R_STEP:R_STEP + TILES]
            link(dve.tensor_tensor(eq, incl[:, :, TILES - 1:TILES].to_broadcast([P, E, TILES]), per_t(first_slots), ALU.is_gt))
            link(dve.tensor_reduce(tiles_e, eq, AX.X, ALU.add))
            link(dve.tensor_tensor_scan(tin, rc[:, R_ONES:R_ONES + E], tiles_e, 0.0, ALU.mult, ALU.add))
            link(dve.tensor_tensor(tex, tin, tiles_e, ALU.subtract))
            link(dve.scalar_tensor_tensor(base, tex.unsqueeze(2).to_broadcast([P, E, TILES]), float(SLOTS), base, ALU.mult, ALU.add))
            link(dve.tensor_tensor(flat(pos), ps_b[:, 0, 0:E * TILES], flat(base), ALU.add))
            for c, oh in ((0, oh1), (1, oh2)):
                link(dve.tensor_tensor(eq, oh, pos, ALU.mult))
                link(dve.tensor_reduce(pos_j[:, c * TILES:(c + 1) * TILES], over_e(eq), AX.X, ALU.add))
            link(dve.tensor_copy(pos_i, pos_j))
            link(dve.tensor_scalar(tile_i, pos_i, P.bit_length() - 1, None, ALU.arith_shift_right))
            link(dve.tensor_scalar(slot_i, pos_i, P - 1, None, ALU.bitwise_and))
            link(dve.tensor_copy(tile_f, tile_i))
            link(dve.tensor_copy(slot_f, slot_i))
            for c in range(TOPK * TILES // RG):
                g = slice(c * RG, (c + 1) * RG)
                if c >= 2:
                    dve.wait_ge(rt_grp, c - 1)
                    dve.wait_ge(rt_pos, c - 1)
                dve.tensor_tensor(is_tile[c % 2], count_rep[:, 0:UNITS, :],
                                  tile_f[:, g].unsqueeze(1).to_broadcast([P, UNITS, RG]), ALU.is_equal).then_inc(rt_unit, 1)
                if c >= 2:
                    dve.wait_ge(rt_grp_used, c - 1)
                dve.tensor_tensor(is_slot[c % 2], count_rep, slot_f[:, g].unsqueeze(1).to_broadcast([P, P, RG]),
                                  ALU.is_equal).then_inc(rt_slot, 1)
            link(dve.tensor_tensor(ecmp, tex[:, 1:E].unsqueeze(1).to_broadcast([P, SLOT_TILES, E - 1]),
                                   rc[:, R_IOTA:R_IOTA + SLOT_TILES].unsqueeze(2).to_broadcast([P, SLOT_TILES, E - 1]), ALU.is_le))
            link(dve.tensor_reduce(ecount, ecmp, AX.X, ALU.add))
            link(dve.tensor_copy(slot_expert[:, :], ecount))
            dve.wait_ge(rt_grp_used, TOPK * TILES // RG)
            ps_group, ps_pos = ps_c[:, 0, 0:UNITS], ps_c[:, 0, UNITS:2 * UNITS]
            link(dve.scalar_tensor_tensor(pad_p, ps_group, 0.0, rc[:, R_PAD:R_PAD + UNITS], ALU.is_ge, ALU.mult))
            link(dve.scalar_tensor_tensor(pair_f, ps_group, float(P), pad_p, ALU.mult, ALU.add))
            link(dve.scalar_tensor_tensor(dest_f, ps_pos, float(TOPK * TOKENS), pair_f, ALU.add, ALU.add))
            link(dve.tensor_copy(slot_dest[:, :], dest_f))
            dve.tensor_scalar(slot_token[:, :], slot_dest[:, :], TOKENS - 1, None, ALU.bitwise_and).then_inc(routed, 1)

            dve.wait_ge(routed, 1)

            def moe(j, u):
                k, half, b = here(j, u, 2)
                if moe_valid(k):
                    dve.wait_ge(gt_ps, k + 1)
                    since(dve, h_ps, GQ * (k - 1))
                    src = ps_x[:, b, :].rearrange("p (c n) -> p c n", c=HC)
                    dve.tensor_scalar(xt_hi[b], src, X_SCALE, None, ALU.mult).then_inc(xh_r, 1)
                    dve.wait_ge(xh_r, k + 1)
                    dve.scalar_tensor_tensor(xt_lo[b], src, X_SCALE, xt_hi[b], ALU.mult, ALU.subtract).then_inc(xl_r, 1)
                k, half, b = here(j, u, 1)
                if moe_valid(k):
                    since(dve, y_ps, k - 1)
                    for q in range(GQ):
                        c = slice(q * IC // GQ, (q + 1) * IC // GQ)
                        src = g_s[q].rearrange("p (c n) -> p c n", n=SLOTS)
                        dve.wait_ge(g_r, GQ * k + 1 + q)
                        dve.tensor_scalar(g_hi[b][:, c, :], src, G_SCALE, None, ALU.mult).then_inc(gh_r, 1)
                        dve.wait_ge(gh_r, GQ * k + 1 + q)
                        dve.scalar_tensor_tensor(g_lo[b][:, c, :], src, G_SCALE, g_hi[b][:, c, :], ALU.mult, ALU.subtract).then_inc(gl_r, 1)
            moe(-1, 0)
            moe(-1, 1)
            moe_steps(dve, 0, moe)

            def group(g, j, u):
                at_g = g - 3
                if group_valid(at_g):
                    dve.wait_ge(c_rsr, at_g + 1)
                    dve.scalar_tensor_tensor(c_nm[:, bass.ds(CG * at_g, CG)].unsqueeze(2), c_mv[(u - 3) % 4][:, :, 0:1], -1.0,
                                             c_rs[:, bass.ds(CG * at_g, CG)].unsqueeze(2), ALU.mult, ALU.mult).then_inc(c_nmr, 1)
                if group_valid(g):
                    for r in range(CG):
                        t = CG * g + r
                        dve.wait_ge(c_f0, t + 1)
                        dve.scalar_tensor_tensor(f_s[:, bass.ds(t, 1), :].rearrange("p a d -> p (a d)"),
                                                 y_in[:, bass.ds(g, 1), 1, r * D:(r + 1) * D].rearrange("p a d -> p (a d)"),
                                                 mix_w[:, 1, bass.ds(t, 1)],
                                                 f_s[:, bass.ds(t, 1), :].rearrange("p a d -> p (a d)"), ALU.mult, ALU.add).then_inc(c_f1, 1)
                    for r in range(CG):
                        t = CG * g + r
                        since(dve, c_mvr, CG * (g - 3))
                        dve.wait_ge(c_f1, t + 1)
                        settled(dve)
                        dve.bn_stats(c_st[u][:, r, :],
                                     f_s[:, bass.ds(t, 1), :].rearrange("p a d -> p (a d)")).then_inc(c_stats, 1)
                at_g = g - 1
                if group_valid(at_g):
                    since(dve, c_nmr, at_g - 1)
                    for r in range(CG):
                        dve.wait_ge(c_stats, CG * at_g + r + 1)
                        settled(dve)
                        dve.bn_aggr(c_mv[(u - 1) % 4][:, r, :], c_st[(u - 1) % 4][:, r, :]).then_inc(c_mvr, 1)
            group_steps(dve, group)

        @block.scalar
        def _(act):
            act.dma_start(cst[:, :], small).then_inc(small_in, 16)
            act.dma_start(w_qk_s, w_qk).then_inc(qk_in, 16)
            act.dma_start(wv_flat, w_vo[:, 0:HC * D]).then_inc(rest_in, 16)
            act.dma_start(wo_flat, w_vo[:, HC * D:2 * HC * D]).then_inc(rest_in, 16)
            act.dma_start(bo_s, bo).then_inc(rest_in, 16)
            act.wait_ge(small_in, 16)
            act.wait_ge(zeroed, 4)

            def step(j, u):
                t, half, b = here(j, u, 1)
                if valid(t):
                    act.wait_ge(xt_ps, t + 1)
                    since(act, k_ps, t)
                    since(act, lg_ps, t - 4)
                    act.activation(xn_t, ps_xt, ACT.Copy).then_inc(xt_r, 1)
                t, half, b = here(j, u, 0)
                if valid(t):
                    act.wait_ge(ctx_in[b], 16 * (half + 1))
                    act.wait_ge(k_ps, t + 1)
                    act.activation(ctx[b], ctx[b], ACT.Copy, scale=CTX_SCALE).then_inc(ctx_scaled, 1)
                t, half, b = here(j, u, 0)
                if valid(t):
                    act.wait_ge(w_in[b], 16 * (half + 1))
                    act.activation(staging[b], staging[b], ACT.Copy, scale=W_SCALE).then_inc(w_scaled, 1)
                t, half, b = here(j, u, -1)
                if valid(t):
                    act.wait_ge(pt_ps, t + 1)
                    since(act, o_ps, t)
                    act.activation(prob_t, ps_pt, ACT.Copy).then_inc(pt_r, 1)
                t, half, b = here(j, u, 0)
                if valid(t):
                    act.wait_ge(ctx_scaled, t + 1)
                    since(act, v_ps, t)
                    since(act, ctx_lo_r, t)
                    act.activation(ctx_hi, ctx[b], ACT.Copy).then_inc(ctx_hi_r, 1)
                t, half, b = here(j, u, 0)
                if valid(t):
                    act.wait_ge(w_scaled, t + 1)
                    act.activation(w_hi[:, bass.ds(t * WCOLS, WCOLS)], staging[b], ACT.Copy).then_inc(w_hi_r, 1)
                t, half, b = here(j, u, 0)
                if valid(t):
                    act.wait_ge(sub_r, t + 1)
                    act.activation(prob, prob, ACT.Exp, scale=DK ** -0.5).then_inc(p_r, 1)
                t, half, b = here(j, u, -2)
                if valid(t):
                    act.wait_ge(ot_ps, t + 1)
                    since(act, wo_ps, t)
                    for h in range(2):
                        act.activation(o_t[:, h, :].rearrange("p (b q) -> p b q", b=NB), ps_ot[:, :, h * BLOCK:(h + 1) * BLOCK],
                                       ACT.Identity, bias=bv_s[:, h:h + 1]).then_inc(ot_r, 1)
                t, half, b = here(j, u, -3)
                if valid(t):
                    act.wait_ge(x2t_ps, t + 1)
                    if valid(t + 3):
                        act.wait_ge(v_ps, t + 4)
                    since(act, lg_ps, t)
                    act.activation(xn2_t, ps_x2t, ACT.Copy).then_inc(x2t_r, 1)
                t, half, b = here(j, u, 0)
                if valid(t):
                    act.wait_ge(v_ps, t + 1)
                    since(act, o_ps, t - 1)
                    for n in range(NB):
                        r = slice(n * BLOCK, (n + 1) * BLOCK)
                        act.activation(v_x[b][r, :, :, n, 0:2 * DK],
                                       ps_v[r].rearrange("p (c s d) -> p s c d", c=HC, s=STRIPS),
                                       ACT.Copy, scale=1.0 / (CTX_SCALE * W_SCALE)).then_inc(v_r, 1)
            step(-1, 1)
            act.wait_ge(rest_in, 48)
            act.activation(wv_s, wv_s, ACT.Copy, scale=W_SCALE).then_inc(wv_scaled, 1)
            act.wait_ge(wv_scaled, 1)
            act.activation(wv_hi, wv_s, ACT.Copy).then_inc(wv_hi_r, 1)
            act.wait_ge(wv_lo_r, 1)
            steps(act, 0, step)

            act.wait_ge(rt_shifted, 1)
            act.activation(ex, lg_s, ACT.Exp).then_inc(rt_exp, 1)
            for c in range(TOPK * TILES // RG):
                act.wait_ge(rt_unit, c + 1)
                if c >= 2:
                    act.wait_ge(rt_grp_used, c - 1)
                act.activation(tile_val[c % 2][:, 1], is_tile[c % 2], ACT.Copy, scale=rc[:, R_P:R_P + 1]).then_inc(rt_pos, 1)
            act.activation(warm[:, :], eps[:, 0:1], ACT.Gelu)
            act.wait_ge(routed, 1)

            def moe(j, u):
                k, half, b = here(j, u, 1)
                if moe_valid(k):
                    for q in range(GQ):
                        act.wait_ge(h_ps, GQ * k + 1 + q)
                        since(act, gl_r, GQ * (k - 1) + 1 + q)
                        act.activation(g_s[q], ps_h[:, q, :], ACT.Gelu, scale=1.0 / (X_SCALE * W_SCALE)).then_inc(g_r, 1)
                k, half, b = here(j, u, 0)
                if moe_valid(k):
                    act.wait_ge(y_ps, k + 1)
                    since(act, scat[b], 16 * SUBS * half)
                    act.activation(y_s[b], ps_y[:, b, :], ACT.Copy, scale=1.0 / (G_SCALE * W_SCALE)).then_inc(y_r, 1)
            moe(-1, 1)
            moe_steps(act, 0, moe)

            def group(g, j, u):
                if group_valid(g):
                    act.wait_ge(yin[u], 16 * TOPK * (j + 1))
                    for r in range(CG):
                        t = CG * g + r
                        act.activation(f_s[:, bass.ds(t, 1), :].rearrange("p a d -> p (a d)"),
                                       y_in[:, bass.ds(g, 1), 0, r * D:(r + 1) * D].rearrange("p a d -> p (a d)"),
                                       ACT.Copy, scale=mix_w[:, 0, bass.ds(t, 1)]).then_inc(c_f0, 1)
                g = g - 3
                if group_valid(g):
                    act.wait_ge(c_nmr, g + 1)
                    for r in range(CG):
                        t = CG * g + r
                        act.activation(o_s[:, bass.ds(t, 1), :].rearrange("p a d -> p (a d)"),
                                       f_s[:, bass.ds(t, 1), :].rearrange("p a d -> p (a d)"),
                                       ACT.Identity, bias=c_nm[:, bass.ds(t, 1)], scale=c_rs[:, bass.ds(t, 1)]).then_inc(c_ap, 1)
            group_steps(act, group)

        @block.gpsimd
        def _(pool):
            pool.memset(neg_half[:, :], -0.5).then_inc(power_r, 1)
            pool.memset(eps[:, :], LN_EPS).then_inc(power_r, 1)
            pool.wait_ge(power_r, 2)

            def rstd(t, mv, ve, ve_r, rs, rs_r):
                pool.tensor_tensor(ve, mv[:, 1:2], eps[:, 0:1], ALU.add).then_inc(ve_r, 1)
                pool.wait_ge(ve_r, t + 1)
                pool.tensor_tensor(rs, ve, neg_half[:, 0:1], ALU.pow).then_inc(rs_r, 1)

            def step(j, u):
                t, half, b = here(j, u, -3)
                if valid(t):
                    pool.wait_ge(mv2_r, t + 1)
                    since(pool, rs2_r, t)
                    since(pool, xn2_r, t - 1)
                    rstd(t, mv2[b], ve2, ve2_r, rs2[b], rs2_r)
                t, half, b = here(j, u, 3)
                if valid(t):
                    pool.wait_ge(mv1_r, t + 1)
                    since(pool, xn_r, t - 1)
                    since(pool, rs1_r, t)
                    rstd(t, mv1[b], ve1, ve1_r, rs1[b], rs1_r)
                t, half, b = here(j, u, 1)
                if valid(t):
                    if isinstance(t, int) and t == 0:
                        pool.wait_ge(rest_in, 48)
                    pool.wait_ge(xn_r, t + 1)
                    r = resid[:, bass.ds(t, 1), :].rearrange("p a d -> p (a d)")
                    pool.tensor_tensor(r, r, bo_s, ALU.add).then_inc(bo_added, 1)
                t, half, b = here(j, u, 0)
                if valid(t):
                    pool.wait_ge(ctx_hi_r, t + 1)
                    since(pool, v_ps, t)
                    pool.tensor_tensor(ctx_lo, ctx[b], ctx_hi, ALU.subtract).then_inc(ctx_lo_r, 1)
                t, half, b = here(j, u, 1)
                if valid(t):
                    if isinstance(t, int) and t == 0:
                        pool.wait_ge(small_in, 16)
                    pool.wait_ge(qb_r, t + 1)
                    since(pool, s_ps, t)
                    pool.tensor_tensor(q_m.rearrange("p c b h q -> p (c b) h q"),
                                       q_b.rearrange("p c (b q) -> p (c b) q", b=NB).unsqueeze(2).to_broadcast([P, HC * NB, 2, BLOCK]),
                                       cst[:, C_MASK:C_MASK + 2].unsqueeze(1).unsqueeze(3).to_broadcast([P, HC * NB, 2, BLOCK]),
                                       ALU.mult).then_inc(q_r, 1)
                t, half, b = here(j, u, 0)
                if valid(t):
                    cols = bass.ds(t * WCOLS, WCOLS)
                    pool.wait_ge(w_hi_r, t + 1)
                    pool.tensor_tensor(w_lo[:, cols], staging[b], w_hi[:, cols], ALU.subtract).then_inc(w_lo_r, 1)
                t, half, b = here(j, u, -3)
                if valid(t):
                    pool.wait_ge(xn2_r, t + 1)
                    r = resid[:, bass.ds(t, 1), :].rearrange("p a d -> p (a d)")
                    pool.tensor_tensor(r, r, xn2, ALU.add).then_inc(xn2_added, 1)
            for i in range(-3, 0):
                step(i // 2, i % 2)
            steps(pool, 0, step)

            for c in range(TOPK * TILES // RG):
                pool.wait_ge(rt_unit, c + 1)
                if c >= 2:
                    pool.wait_ge(rt_grp_used, c - 1)
                pool.tensor_tensor(tile_val[c % 2][:, 0], is_tile[c % 2],
                                   rc[:, R_GRP + c * RG:R_GRP + (c + 1) * RG].unsqueeze(1).to_broadcast([P, UNITS, RG]),
                                   ALU.mult).then_inc(rt_grp, 1)

            pool.wait_ge(routed, 1)
            for b in range(2):
                pool.wait_ge(xn2_out[b], 16 * TILES // 2)

            def moe(j, u):
                k, half, b = here(j, u, 3)
                if moe_valid(k):
                    since(pool, gt_ps, k - 1)
                    since(pool, gat[b], 16 * SUBS * half)
                    pool.tensor_copy(gidx[b], slot_token[:, bass.ds(SUBS * k, SUBS)]).then_inc(gidx_r, 1)
                    pool.wait_ge(gidx_r, k + 1)
                    settled(pool)
                    for v in range(SUBS):
                        pool.indirect_dma_start(xg[b][:, v, :], None, xn_rows[:, :],
                                                bass.IndirectOffsetOnAxis(ap=gidx[b][:, v:v + 1], axis=0)).then_inc(gat[b], 16)
                k, half, b = here(j, u, -1)
                if moe_valid(k):
                    since(pool, scat[b], 16 * SUBS * half)
                    pool.tensor_copy(didx[b], slot_dest[:, bass.ds(SUBS * k, SUBS)]).then_inc(didx_r, 1)
                    pool.wait_ge(didx_r, k + 1)
                    pool.wait_ge(y_r, k + 1)
                    settled(pool)
                    for v in range(SUBS):
                        pool.indirect_dma_start(y_rows[:, :], bass.IndirectOffsetOnAxis(ap=didx[b][:, v:v + 1], axis=0),
                                                y_s[b][:, v * D:(v + 1) * D], None).then_inc(scat[b], 16)
            for k in range(-3, 0):
                moe(k // 2, k % 2)
            moe_steps(pool, 0, moe)

            def group(g, j, u):
                at_g = g - 4
                if group_valid(at_g):
                    r = bass.ds(CG * at_g, CG)
                    pool.wait_ge(c_ap, CG * (at_g + 1))
                    pool.tensor_tensor(o_s[:, r, :], o_s[:, r, :], resid[:, r, :], ALU.add).then_inc(c_out, 1)
                at_g = g - 1
                if group_valid(at_g):
                    r = bass.ds(CG * at_g, CG)
                    pool.wait_ge(c_mvr, CG * (at_g + 1))
                    pool.tensor_tensor(c_ve[:, r].unsqueeze(2), c_mv[(u - 1) % 4][:, :, 1:2], eps[:, :].unsqueeze(2), ALU.add).then_inc(c_ver, 1)
                    pool.wait_ge(c_ver, at_g + 1)
                    pool.tensor_tensor(c_rs[:, r], c_ve[:, r], neg_half[:, :], ALU.pow).then_inc(c_rsr, 1)
            group_steps(pool, group)


def kernel(x, ctx_1024, L0_xattn_Wq, L0_xattn_bq, L0_xattn_Wk, L0_xattn_bk, L0_xattn_Wv, L0_xattn_bv, L0_xattn_Wo, L0_xattn_bo,
           L0_ffn_gate_w, L0_ffn_expert_bias, L0_ffn_w_up, L0_ffn_w_down):
    import concourse.bacc as bacc
    from concourse.bass_utils import run_bass_kernel_spmd

    rows = lambda w: np.asarray(w).reshape(HC, P, -1).transpose(1, 0, 2)
    heads = (HC, STRIPS, 2, DK)
    up = np.asarray(L0_ffn_w_up).transpose(0, 2, 1).reshape(E, HC, P, I)
    down = np.asarray(L0_ffn_w_down).transpose(0, 2, 1).reshape(E, 2, IC // 2, P, D).transpose(0, 1, 3, 2, 4).reshape(E, 2, P, WCOLS)
    wo = np.asarray(L0_xattn_Wo).reshape(*heads, D).transpose(1, 0, 3, 2, 4).reshape(P, 2, D)
    consts, route_consts = constants()
    arrays = {
        "x_in": np.asarray(x).reshape(TILES, P, D),
        "ctx_t": np.asarray(ctx_1024).reshape(TILES, P, HC, P).transpose(0, 3, 2, 1),
        "w_qk": np.concatenate([rows(L0_xattn_Wq), rows(L0_xattn_Wk)], 1).reshape(P, -1),
        "w_vo": np.concatenate([rows(L0_xattn_Wv), wo], 1).reshape(P, -1),
        "bo": np.broadcast_to(np.asarray(L0_xattn_bo), (P, D)),
        "weights": np.concatenate([up, down], 1).reshape(WSTEPS, P, WCOLS),
        "small": np.concatenate([consts, np.asarray(L0_xattn_bq).reshape(HC, P).T, np.asarray(L0_xattn_bk).reshape(HC, P).T,
                                 np.asarray(L0_xattn_bv).reshape(heads).transpose(1, 0, 3, 2).reshape(P, 2),
                                 rows(np.asarray(L0_ffn_gate_w).T).reshape(P, HC * E),
                                 np.broadcast_to(np.asarray(L0_ffn_expert_bias), (P, E))], 1),
        "route_consts": route_consts,
    }
    arrays = {n: np.ascontiguousarray(a) for n, a in arrays.items()}
    nc = bacc.Bacc("TRN2", target_bir_lowering=False, num_devices=1)
    args = [nc.dram_tensor(n, a.shape, mybir.dt.from_np(a.dtype), kind="ExternalInput").ap() for n, a in arrays.items()]
    out = nc.dram_tensor("out", (TILES, P, D), F32, kind="ExternalOutput").ap()
    program(nc, *args, out)
    r = run_bass_kernel_spmd(nc, [arrays], core_ids=[0])
    return r.results[0]["out"].reshape(BATCH, SEQ, D)
```
